# Optimizing a Trainium2 kernel written in Bass

```python
import numpy as np
import jax
import jax.numpy as jnp

def _softmax(x, axis=-1):
    return jax.nn.softmax(x, axis=axis)
def _gelu(x):
    return jax.nn.gelu(x, approximate=True)
def _silu(x):
    return jax.nn.silu(x)
def _sigmoid(x):
    return jax.nn.sigmoid(x)
def _layernorm(x, axis=-1, eps=1e-5):
    m = jnp.mean(x, axis=axis, keepdims=True)
    v = jnp.var(x, axis=axis, keepdims=True)
    return (x - m) / jnp.sqrt(v + eps)
def _scatter_add(tgt, idx, src, axis=0):
    return tgt.at[idx].add(src)
def _segment_sum(src, seg, n):
    return jax.ops.segment_sum(src, seg, n)

kernel_name = 'mk_conv_seq_d2_conv_nchw1024_62cbb2'

def setup_inputs(seed: int = 0):
    np.random.seed(seed)
    _w = jnp.asarray
    def _rec_inputs():
        import jax
        import jax.numpy as jnp
        _gk = jax.random.key(seed)
        x = -0.0003957 + 1 * jax.random.normal(jax.random.fold_in(_gk, 1), (64, 1024, 14, 14), jnp.float32)
        return x
    x = _rec_inputs()
    def _L0_conv_setup():
        import jax, jax.numpy as jnp
        import numpy as np
        EPS = 1e-05

        def _conv(x, w, b, stride, pad):
            y = jax.lax.conv_general_dilated(x, w, window_strides=(stride, stride), padding=[(pad, pad), (pad, pad)], dimension_numbers=('NCHW', 'OIHW', 'NCHW'))
            return y + b.reshape(1, -1, 1, 1)

        def _bn(x, gamma, beta):
            mean = jnp.mean(x, axis=(0, 2, 3), keepdims=True)
            var = jnp.var(x, axis=(0, 2, 3), keepdims=True)
            xn = (x - mean) * jax.lax.rsqrt(var + EPS)
            return gamma.reshape(1, -1, 1, 1) * xn + beta.reshape(1, -1, 1, 1)
        key = jax.random.key(seed)
        ks = jax.random.split(key, 8)
        N, Cin, H, W = (64, 1024, 14, 14)
        P = 256
        Cout = P * 4

        def kaiming(k, shape):
            fan_in = shape[1] * shape[2] * shape[3]
            return jax.random.normal(k, shape, jnp.float32) * np.float32(np.sqrt(2.0 / fan_in))
        return {'x': jax.random.normal(ks[0], (N, Cin, H, W), jnp.float32), 'w1': kaiming(ks[1], (P, Cin, 1, 1)), 'b1': jnp.zeros((P,), jnp.float32), 'g1': jnp.ones((P,), jnp.float32), 'be1': jnp.zeros((P,), jnp.float32), 'w2': kaiming(ks[2], (P, P, 3, 3)), 'b2': jnp.zeros((P,), jnp.float32), 'g2': jnp.ones((P,), jnp.float32), 'be2': jnp.zeros((P,), jnp.float32), 'w3': kaiming(ks[3], (Cout, P, 1, 1)), 'b3': jnp.zeros((Cout,), jnp.float32), 'g3': jnp.ones((Cout,), jnp.float32), 'be3': jnp.zeros((Cout,), jnp.float32), 'residual_scale': jnp.zeros((1,), jnp.float32)}
    _L0_conv_all = _L0_conv_setup()
    _L0_conv_in = {k: v for k, v in _L0_conv_all.items() if k in ('w1', 'b1', 'g1', 'be1', 'w2', 'b2', 'g2', 'be2', 'w3', 'b3', 'g3', 'be3', 'residual_scale', )}
    del _L0_conv_all

    def _L1_conv_setup():
        import jax, jax.numpy as jnp
        import numpy as np
        NUM_MODELS = 64
        IN_CHANNELS = 16
        HIDDEN = 128
        B, H, W = (16, 32, 32)

        def _perceive(x):
            b, mc, h, w = x.shape
            padded = jnp.pad(x, ((0, 0), (0, 0), (1, 1), (1, 1)))
            shifts = [x]
            for r in (-1, 0, 1):
                for c in (-1, 0, 1):
                    if r == 0 and c == 0:
                        continue
                    shifts.append(padded[:, :, r + 1:r + 1 + h, c + 1:c + 1 + w])
            return jnp.concatenate(shifts, axis=1)
        key = jax.random.key(seed)
        k1, k2, k3, k4, k5 = jax.random.split(key, 5)
        M, C, Hd = (NUM_MODELS, IN_CHANNELS, HIDDEN)
        x = jax.random.normal(k1, (B, M * C, H, W), dtype=jnp.float32)
        w1 = jax.random.normal(k2, (M, Hd, 9 * C), dtype=jnp.float32) * 0.05
        b1 = jax.random.normal(k3, (M * Hd,), dtype=jnp.float32) * 0.05
        w2 = jax.random.normal(k4, (M, C, Hd), dtype=jnp.float32) * 0.05
        b2 = jax.random.normal(k5, (M * C,), dtype=jnp.float32) * 0.05
        return {'x': x, 'w1': w1, 'b1': b1, 'w2': w2, 'b2': b2}
    _L1_conv_all = _L1_conv_setup()
    _L1_conv_in = {k: v for k, v in _L1_conv_all.items() if k in ('w1', 'b1', 'w2', 'b2', )}
    del _L1_conv_all

    return {
        "x": x,
        "L0_conv_w1": _L0_conv_in["w1"],
        "L0_conv_b1": _L0_conv_in["b1"],
        "L0_conv_g1": _L0_conv_in["g1"],
        "L0_conv_be1": _L0_conv_in["be1"],
        "L0_conv_w2": _L0_conv_in["w2"],
        "L0_conv_b2": _L0_conv_in["b2"],
        "L0_conv_g2": _L0_conv_in["g2"],
        "L0_conv_be2": _L0_conv_in["be2"],
        "L0_conv_w3": _L0_conv_in["w3"],
        "L0_conv_b3": _L0_conv_in["b3"],
        "L0_conv_g3": _L0_conv_in["g3"],
        "L0_conv_be3": _L0_conv_in["be3"],
        "L0_conv_residual_scale": _L0_conv_in["residual_scale"],
        "L1_conv_w1": _L1_conv_in["w1"],
        "L1_conv_b1": _L1_conv_in["b1"],
        "L1_conv_w2": _L1_conv_in["w2"],
        "L1_conv_b2": _L1_conv_in["b2"],
    }

def reference(x, L0_conv_w1, L0_conv_b1, L0_conv_g1, L0_conv_be1, L0_conv_w2, L0_conv_b2, L0_conv_g2, L0_conv_be2, L0_conv_w3, L0_conv_b3, L0_conv_g3, L0_conv_be3, L0_conv_residual_scale, L1_conv_w1, L1_conv_b1, L1_conv_w2, L1_conv_b2):
    import jax
    import jax.numpy as jnp
    def _L0_conv_ref(x, w1, b1, g1, be1, w2, b2, g2, be2, w3, b3, g3, be3, residual_scale):
        import jax, jax.numpy as jnp
        import numpy as np
        EPS = 1e-05

        def _conv(x, w, b, stride, pad):
            y = jax.lax.conv_general_dilated(x, w, window_strides=(stride, stride), padding=[(pad, pad), (pad, pad)], dimension_numbers=('NCHW', 'OIHW', 'NCHW'))
            return y + b.reshape(1, -1, 1, 1)

        def _bn(x, gamma, beta):
            mean = jnp.mean(x, axis=(0, 2, 3), keepdims=True)
            var = jnp.var(x, axis=(0, 2, 3), keepdims=True)
            xn = (x - mean) * jax.lax.rsqrt(var + EPS)
            return gamma.reshape(1, -1, 1, 1) * xn + beta.reshape(1, -1, 1, 1)
        out = jax.nn.relu(_bn(_conv(x, w1, b1, 1, 0), g1, be1))
        out = jax.nn.relu(_bn(_conv(out, w2, b2, 1, 1), g2, be2))
        out = _bn(_conv(out, w3, b3, 1, 0), g3, be3)
        out = jax.nn.softplus(residual_scale)[0] * out
        out = x + out
        return jax.nn.relu(out)

    def _L1_conv_ref(x, w1, b1, w2, b2):
        import jax, jax.numpy as jnp
        import numpy as np
        NUM_MODELS = 64
        IN_CHANNELS = 16
        HIDDEN = 128
        B, H, W = (16, 32, 32)

        def _perceive(x):
            b, mc, h, w = x.shape
            padded = jnp.pad(x, ((0, 0), (0, 0), (1, 1), (1, 1)))
            shifts = [x]
            for r in (-1, 0, 1):
                for c in (-1, 0, 1):
                    if r == 0 and c == 0:
                        continue
                    shifts.append(padded[:, :, r + 1:r + 1 + h, c + 1:c + 1 + w])
            return jnp.concatenate(shifts, axis=1)
        M, C, Hd = (NUM_MODELS, IN_CHANNELS, HIDDEN)
        b, _, h, w = x.shape
        perception = _perceive(x)
        per_g = perception.reshape(b, M, 9 * C, h, w)
        hdn = jnp.einsum('bmchw,mdc->bmdhw', per_g, w1) + b1.reshape(1, M, Hd, 1, 1)
        hdn = jax.nn.relu(hdn)
        dx = jnp.einsum('bmdhw,mcd->bmchw', hdn, w2) + b2.reshape(1, M, C, 1, 1)
        return x + dx.reshape(b, M * C, h, w)

    def _gn(v, G=32, eps=1e-5):
        B_, C_, H_, W_ = v.shape
        g = v.reshape(B_, G, C_ // G, H_, W_)
        m = jnp.mean(g, axis=(2, 3, 4), keepdims=True)
        s = jnp.var(g, axis=(2, 3, 4), keepdims=True)
        return ((g - m) / jnp.sqrt(s + eps)).reshape(v.shape)

    def _ln_c(v, eps=1e-6):
        m = jnp.mean(v, axis=1, keepdims=True)
        s = jnp.var(v, axis=1, keepdims=True)
        return (v - m) / jnp.sqrt(s + eps)

    def _ln_t(v, eps=1e-5):
        m = jnp.mean(v, axis=-1, keepdims=True)
        s = jnp.var(v, axis=-1, keepdims=True)
        return (v - m) / jnp.sqrt(s + eps)

    def _to_tokens(v):
        B_, C_, H_, W_ = v.shape
        return v.reshape(B_, C_, H_ * W_).transpose(0, 2, 1)
    def _from_tokens(t, like):
        B_, C_, H_, W_ = like.shape
        return t.transpose(0, 2, 1).reshape(B_, C_, H_, W_)

    x = _L0_conv_ref(x, L0_conv_w1, L0_conv_b1, L0_conv_g1, L0_conv_be1, L0_conv_w2, L0_conv_b2, L0_conv_g2, L0_conv_be2, L0_conv_w3, L0_conv_b3, L0_conv_g3, L0_conv_be3, L0_conv_residual_scale)
    x = _L1_conv_ref(x, L1_conv_w1, L1_conv_b1, L1_conv_w2, L1_conv_b2)
    return x


_drawn_inputs = setup_inputs


def setup_inputs(seed=0):
    import zlib

    import numpy as np

    out = dict(_drawn_inputs(seed))
    spreads = {'L0_conv_b1': (0.0, 0.1),
     'L0_conv_g1': (1.0, 0.2),
     'L0_conv_be1': (0.0, 0.1),
     'L0_conv_b2': (0.0, 0.1),
     'L0_conv_g2': (1.0, 0.2),
     'L0_conv_be2': (0.0, 0.1),
     'L0_conv_b3': (0.0, 0.1),
     'L0_conv_g3': (1.0, 0.2),
     'L0_conv_be3': (0.0, 0.1)}
    factors = {}
    for name, (base, spread) in spreads.items():
        noise = np.random.default_rng([zlib.crc32(name.encode()), seed]).standard_normal(out[name].shape)
        drawn = base * np.exp(spread * noise) if base else spread * noise
        out[name] = jnp.asarray(drawn.astype(out[name].dtype))
    for name, factor in factors.items():
        out[name] = (out[name] * factor).astype(out[name].dtype)
    return out
```

```python
from contextlib import ExitStack

import numpy as np

import concourse.bass as bass
from concourse import mybir

F32 = mybir.dt.float32
F32R = mybir.dt.float32r
ACT = mybir.ActivationFunctionType
ALU = mybir.AluOpType

P = 128
N_IMG, C_IN, H, W = 64, 1024, 14, 14
C_MID = 256
PAIRS = N_IMG // 2
COLS = 2 * H * W
T = N_IMG * H * W
PAD = 2 * (H + 2) * (W + 2)
KT = C_IN // P
MT = C_MID // P
BODIES = PAIRS // 2
TAPS = [(r, c) for r in (-1, 0, 1) for c in (-1, 0, 1)]
BN_EPS = 1e-5

GROUPS, GC, HID = 64, 16, 128
SHIFTS = [(0, 0)] + [t for t in TAPS if t != (0, 0)]
PASSES = 4
WPP = GROUPS // PASSES
WT = 3
OCT = 8
LAG = 3
HB = 4


def group_of(k):
    return pow(9, -1, GROUPS) * k % GROUPS


def shift_of(k, tile):
    s = (9 * group_of(k) * GC) // C_IN
    return s + 1 if tile and k // OCT + 1 == KT else s


PARAMS = {}
_at = 0
for _name, _n in (("b1", MT), ("g1", MT), ("be1", MT), ("b2", MT), ("g2", MT), ("be2", MT),
                  ("b3", KT), ("g3", KT), ("be3", KT), ("rs", 1), ("hid_b", GROUPS), ("out_b", KT)):
    PARAMS[_name] = (_at, _at + _n)
    _at += _n
N_PARAMS = _at


def build(nc, x, w1, w2, w3, wmain, wside, wout_a, wout_b, params, out):
    y3 = nc.dram_tensor("y3_spill", [C_IN, T], F32).ap()
    x_t = x.rearrange("(t p) n -> p t n", p=P)
    y3_t = y3.rearrange("(t p) n -> p t n", p=P)
    out_t = out.rearrange("(t p) n -> p t n", p=P)

    with ExitStack() as ctx:
        par = ctx.enter_context(nc.sbuf_tensor("par", [P, N_PARAMS], F32))
        coef = ctx.enter_context(nc.sbuf_tensor("coef", [P, KT, 2], F32))
        mv = ctx.enter_context(nc.sbuf_tensor("mv", [P, KT, 2], F32))
        tmp = ctx.enter_context(nc.sbuf_tensor("tmp", [P, 4, KT], F32))
        sp = ctx.enter_context(nc.sbuf_tensor("sp", [P, 8], F32))
        par_in = ctx.enter_context(nc.semaphore("par_in"))

        def pv(name):
            a, b = PARAMS[name]
            return par[:, a:b]

        with ExitStack() as mid:
            y = mid.enter_context(nc.sbuf_tensor("y", [P, MT, T], F32))
            stats = mid.enter_context(nc.sbuf_tensor("stats", [P, MT, PAIRS, 6], F32))
            stats3 = mid.enter_context(nc.sbuf_tensor("stats3", [P, KT, PAIRS, 6], F32))
            conv1(nc, x_t, w1, y, stats, par, params, par_in)
            conv2(nc, w2, y, stats, mv, tmp, coef, pv, sp, par_in)
            conv3(nc, w3, y, stats, stats3, mv, tmp, coef, pv, y3_t)
        layer1(nc, x, x_t, y3, y3_t, out_t, wmain, wside, wout_a, wout_b, mv, tmp, coef, pv, sp)


def split(nc, dve, hi, lo, v, done, count):
    nc.vector.tensor_copy(hi, v).then_inc(done, 1)
    dve.wait_ge(done, count + 1)
    nc.vector.tensor_tensor(lo, v, hi.bitcast(F32), ALU.subtract).then_inc(done, 1)
    return count + 2


def bn_coefficients(nc, dve, step, count, scale, shift, mv, tmp, b, g, be, n, sqrt_in, sqrt_out, by=None):
    def then(ins):
        nonlocal count
        count += 1
        ins.then_inc(step, 1)
        dve.wait_ge(step, count)

    mean, var = mv[:, 0:n, 0], mv[:, 0:n, 1]
    v, r, e, m = (tmp[:, i, 0:n] for i in range(4))
    then(nc.vector.tensor_tensor(m, mean, b, ALU.add))
    nc.vector.tensor_scalar(v, var, BN_EPS, None, ALU.add).then_inc(sqrt_in, 1)
    dve.wait_ge(sqrt_out, 1)
    then(nc.vector.reciprocal(r, r))
    then(nc.vector.tensor_tensor(e, v, r, ALU.mult))
    then(nc.vector.tensor_tensor(e, e, r, ALU.mult))
    then(nc.vector.tensor_scalar(e, e, -0.5, 1.5, ALU.mult, ALU.add))
    then(nc.vector.tensor_tensor(r, r, e, ALU.mult))
    then(nc.vector.tensor_tensor(scale, r, g, ALU.mult))
    then(nc.vector.tensor_tensor(m, b, m, ALU.subtract))
    then(nc.vector.tensor_tensor(m, m, scale, ALU.mult))
    then(nc.vector.tensor_tensor(shift, m, be, ALU.add))
    if by is not None:
        then(nc.vector.tensor_scalar(scale, scale, by, None, ALU.mult))
        then(nc.vector.tensor_scalar(shift, shift, by, None, ALU.mult))
    return count


def over_bodies(engine, body):
    with engine.Fori(0, BODIES - 1) as i:
        body(i, False)
    body(BODIES - 1, True)


def conv1(nc, x_t, w1, y, stats, par, params, par_in):
    with ExitStack() as c:
        sb = lambda name, shape, dt: c.enter_context(nc.sbuf_tensor(name, shape, dt))
        sem = lambda name: c.enter_context(nc.semaphore(name))
        w_f = sb("a_w", [P, KT, C_MID], F32)
        w_hi = sb("a_w_hi", [P, KT, C_MID], F32R)
        w_lo = sb("a_w_lo", [P, KT, C_MID], F32R)
        x_f = sb("a_x", [P, 2, KT, COLS], F32)
        x_hi = sb("a_x_hi", [P, 2, KT, COLS], F32R)
        x_lo = sb("a_x_lo", [P, 2, KT, COLS], F32R)
        ps = c.enter_context(nc.psum_tensor("a_ps", [P, 4, 512], F32))
        w_in = sem("a_w_in")
        w_split = sem("a_w_split")
        x_in = [sem(f"a_x_in{s}") for s in range(2)]
        hi_done, lo_done = sem("a_hi_done"), sem("a_lo_done")
        conv_done, y_done = sem("a_conv_done"), sem("a_y_done")
        block = c.enter_context(nc.Block())

        @block.sync
        def _(sync):
            sync.dma_start(w_f[:, :, :], w1.rearrange("(t p) m -> p t m", p=P)).then_inc(w_in, 16)

            def load(n, s):
                sync.dma_start(x_f[:, s, :, :], x_t[:, :, bass.ds(n * COLS, COLS)]).then_inc(x_in[s], 16)

            for s in range(2):
                load(s, s)
            sync.dma_start(par[:, :], params).then_inc(par_in, 16)

            def body(i, last):
                for s in range(2):
                    if not last:
                        sync.wait_ge(lo_done, i * 2 + s + 1)
                        load(i * 2 + s + 2, s)

            over_bodies(sync, body)
            sync.wait_ge(par_in, 16)

        @block.scalar
        def _(act):
            def hi(s, uses):
                act.wait_ge(x_in[s], uses * 16)
                nc.scalar.activation(x_hi[:, s, :, :], x_f[:, s, :, :], ACT.Copy).then_inc(hi_done, 1)

            for s in range(2):
                hi(s, 1)

            def body(i, last):
                for s in range(2):
                    for m in range(MT):
                        act.wait_ge(conv_done, i * 4 + 2 * s + m + 1)
                        nc.scalar.activation(y[:, m, bass.ds((i * 2 + s) * COLS, COLS)], ps[:, 2 * s + m, 0:COLS],
                                             ACT.Copy).then_inc(y_done, 1)
                    if not last:
                        hi(s, i + 2)

            over_bodies(act, body)

        @block.vector
        def _(dve):
            dve.wait_ge(w_in, 16)
            split(nc, dve, w_hi[:, :, :], w_lo[:, :, :], w_f[:, :, :], w_split, 0)

            def lo(s, n):
                dve.wait_ge(hi_done, n + 1)
                nc.vector.tensor_tensor(x_lo[:, s, :, :], x_f[:, s, :, :], x_hi[:, s, :, :].bitcast(F32),
                                        ALU.subtract).then_inc(lo_done, 1)

            for s in range(2):
                lo(s, s)

            def body(i, last):
                for s in range(2):
                    for m in range(MT):
                        dve.wait_ge(y_done, i * 4 + 2 * s + m + 1)
                        nc.vector.bn_stats(stats[:, m, bass.ds(i * 2 + s, 1), :].rearrange("p a b -> p (a b)"),
                                           y[:, m, bass.ds((i * 2 + s) * COLS, COLS)])
                    if not last:
                        lo(s, i * 2 + s + 2)

            over_bodies(dve, body)

        @block.tensor
        def _(pe):
            pe.wait_ge(w_split, 2)

            def body(i, last):
                for s in range(2):
                    pe.wait_ge(lo_done, i * 2 + s + 1)
                    for m in range(MT):
                        steps = [(w, v, k) for k in range(KT) for w, v in ((w_hi, x_hi), (w_lo, x_hi), (w_hi, x_lo))]
                        for at, (w, v, k) in enumerate(steps):
                            last_mm = nc.tensor.matmul(ps[:, 2 * s + m, 0:COLS], w[:, k, m * P:(m + 1) * P],
                                                       v[:, s, k, :], start=at == 0, stop=at == len(steps) - 1)
                        last_mm.then_inc(conv_done, 1)

            over_bodies(pe, body)


def conv2(nc, w2, y, stats, mv, tmp, coef, pv, sp, par_in):
    with ExitStack() as c:
        sb = lambda name, shape, dt: c.enter_context(nc.sbuf_tensor(name, shape, dt))
        sem = lambda name: c.enter_context(nc.semaphore(name))
        w_f = sb("b_w", [P, MT, 9, C_MID], F32)
        w_hi = sb("b_w_hi", [P, MT, 9, C_MID], F32R)
        w_lo = sb("b_w_lo", [P, MT, 9, C_MID], F32R)
        z_f = sb("b_z", [P, 2, MT, COLS], F32)
        z_hi = sb("b_z_hi", [P, 2, MT, PAD], F32R)
        z_lo = sb("b_z_lo", [P, 2, MT, PAD], F32R)
        ps = c.enter_context(nc.psum_tensor("b_ps", [P, 4, 512], F32))
        w_in, w_split = sem("b_w_in"), sem("b_w_split")
        sp_step, sp_exp, sp_ln = sem("b_sp_step"), sem("b_sp_exp"), sem("b_sp_ln")
        bn_step, sqrt_in, sqrt_out, bn_done = sem("b_bn_step"), sem("b_sqrt_in"), sem("b_sqrt_out"), sem("b_bn_done")
        z_done, lo_done = sem("b_z_done"), sem("b_lo_done")
        conv_done, y_done = sem("b_conv_done"), sem("b_y_done")
        block = c.enter_context(nc.Block())

        @block.sync
        def _(sync):
            sync.dma_start(w_f[:, :, :, :], w2.rearrange("(t p) a m -> p t a m", p=P)).then_inc(w_in, 16)

        @block.scalar
        def _(act):
            softplus_act(nc, act, sp, sp_step, sp_exp, sp_ln)
            act.wait_ge(sqrt_in, 1)
            nc.scalar.activation(tmp[:, 1, 0:MT], tmp[:, 0, 0:MT], ACT.Sqrt).then_inc(sqrt_out, 1)
            act.wait_ge(bn_done, 1)

            def z(n, s):
                for m in range(MT):
                    src = y[:, m, bass.ds(n * COLS, COLS)]
                    sc, sh = coef[:, m, 0:1], coef[:, m, 1:2]
                    nc.scalar.activation(z_f[:, s, m, :], src, ACT.Relu, bias=sh, scale=sc)
                    nc.scalar.activation(inner(z_hi[:, s, m, :]), rows(src), ACT.Relu, bias=sh,
                                         scale=sc).then_inc(z_done, 1)

            for s in range(2):
                z(s, s)

            def body(i, last):
                for s in range(2):
                    for m in range(MT):
                        act.wait_ge(conv_done, i * 4 + 2 * s + m + 1)
                        nc.scalar.activation(y[:, m, bass.ds((i * 2 + s) * COLS, COLS)], ps[:, 2 * s + m, 0:COLS],
                                             ACT.Copy).then_inc(y_done, 1)
                    if not last:
                        z(i * 2 + s + 2, s)

            over_bodies(act, body)

        @block.vector
        def _(dve):
            dve.wait_ge(par_in, 16)
            softplus_dve(nc, dve, sp, pv("rs"), sp_step, sp_exp, sp_ln)
            step = 0
            for m in range(MT):
                nc.vector.bn_aggr(mv[:, m, :], stats[:, m, :, :].rearrange("p a b -> p (a b)")).then_inc(bn_step, 1)
                step += 1
            dve.wait_ge(bn_step, step)
            step = bn_coefficients(nc, dve, bn_step, step, coef[:, 0:MT, 0], coef[:, 0:MT, 1], mv, tmp,
                                   pv("b1"), pv("g1"), pv("be1"), MT, sqrt_in, sqrt_out)
            nc.vector.memset(z_hi[:, :, :, :].bitcast(F32), 0.0).then_inc(bn_done, 1)
            nc.vector.memset(z_lo[:, :, :, :].bitcast(F32), 0.0).then_inc(w_split, 1)
            dve.wait_ge(w_in, 16)
            split(nc, dve, w_hi[:, :, :, :], w_lo[:, :, :, :], w_f[:, :, :, :], w_split, 1)
            dve.wait_ge(w_split, 3)

            def lo(n, s):
                for m in range(MT):
                    dve.wait_ge(z_done, n * 2 + m + 1)
                    nc.vector.tensor_tensor(inner(z_lo[:, s, m, :]), rows(z_f[:, s, m, :]),
                                            inner(z_hi[:, s, m, :]).bitcast(F32), ALU.subtract).then_inc(lo_done, 1)

            for s in range(2):
                lo(s, s)

            def body(i, last):
                for s in range(2):
                    for m in range(MT):
                        dve.wait_ge(y_done, i * 4 + 2 * s + m + 1)
                        nc.vector.bn_stats(stats[:, m, bass.ds(i * 2 + s, 1), :].rearrange("p a b -> p (a b)"),
                                           y[:, m, bass.ds((i * 2 + s) * COLS, COLS)])
                    if not last:
                        lo(i * 2 + s + 2, s)

            over_bodies(dve, body)

        @block.tensor
        def _(pe):
            pe.wait_ge(w_split, 3)

            def body(i, last):
                for s in range(2):
                    pe.wait_ge(lo_done, i * 4 + 2 * s + MT)
                    for m in range(MT):
                        steps = [(w, v, k, t) for k in range(MT) for t in range(9)
                                 for w, v in ((w_hi, z_hi), (w_lo, z_hi), (w_hi, z_lo))]
                        for at, (w, v, k, t) in enumerate(steps):
                            last_mm = nc.tensor.matmul(ps[:, 2 * s + m, 0:COLS], w[:, k, t, m * P:(m + 1) * P],
                                                       inner(v[:, s, k, :], *TAPS[t]),
                                                       start=at == 0, stop=at == len(steps) - 1)
                        last_mm.then_inc(conv_done, 1)

            over_bodies(pe, body)


def inner(v, r=0, c=0):
    return v.rearrange("p (i h w) -> p i h w", i=2, h=H + 2)[:, :, 1 + r:1 + r + H, 1 + c:1 + c + W]


def rows(v):
    return v.rearrange("p (i h w) -> p i h w", i=2, h=H)


def softplus_dve(nc, dve, sp, rs, step, exp_done, ln_done):
    col = lambda i: sp[:, i:i + 1]
    n = [0]

    def then(ins):
        n[0] += 1
        ins.then_inc(step, 1)
        dve.wait_ge(step, n[0])

    then(nc.vector.tensor_scalar(col(1), rs, -1.0, None, ALU.mult))
    then(nc.vector.tensor_tensor(col(1), col(1), rs, ALU.min))
    dve.wait_ge(exp_done, 1)
    then(nc.vector.tensor_scalar(col(3), col(2), 1.0, None, ALU.add))
    dve.wait_ge(ln_done, 1)
    then(nc.vector.tensor_scalar(col(5), col(3), -1.0, None, ALU.add))
    then(nc.vector.tensor_scalar(col(6), col(5), 0.0, None, ALU.is_equal))
    then(nc.vector.tensor_tensor(col(5), col(5), col(6), ALU.add))
    then(nc.vector.tensor_tensor(col(4), col(4), col(6), ALU.add))
    then(nc.vector.reciprocal(col(5), col(5)))
    then(nc.vector.tensor_tensor(col(4), col(4), col(5), ALU.mult))
    then(nc.vector.tensor_tensor(col(4), col(4), col(2), ALU.mult))
    then(nc.vector.tensor_scalar(col(0), rs, 0.0, None, ALU.max))
    then(nc.vector.tensor_tensor(col(0), col(0), col(4), ALU.add))


def softplus_act(nc, act, sp, step, exp_done, ln_done):
    act.wait_ge(step, 2)
    nc.scalar.activation(sp[:, 2:3], sp[:, 1:2], ACT.Exp).then_inc(exp_done, 1)
    act.wait_ge(step, 3)
    nc.scalar.activation(sp[:, 4:5], sp[:, 3:4], ACT.Ln).then_inc(ln_done, 1)


def conv3(nc, w3, y, stats, stats3, mv, tmp, coef, pv, y3_t):
    with ExitStack() as c:
        sb = lambda name, shape, dt: c.enter_context(nc.sbuf_tensor(name, shape, dt))
        sem = lambda name: c.enter_context(nc.semaphore(name))
        w_f = sb("c_w", [P, MT, C_IN], F32)
        w_hi = sb("c_w_hi", [P, MT, C_IN], F32R)
        w_lo = sb("c_w_lo", [P, MT, C_IN], F32R)
        z_f = sb("c_z", [P, 2, MT, COLS], F32)
        z_hi = sb("c_z_hi", [P, 2, MT, COLS], F32R)
        z_lo = sb("c_z_lo", [P, 2, MT, COLS], F32R)
        y3s = sb("c_y3", [P, 2, KT, COLS], F32)
        ps = c.enter_context(nc.psum_tensor("c_ps", [P, 8, 512], F32))
        w_in, w_split = sem("c_w_in"), sem("c_w_split")
        bn_step, sqrt_in, sqrt_out, bn_done = sem("c_bn_step"), sem("c_sqrt_in"), sem("c_sqrt_out"), sem("c_bn_done")
        z_done, lo_done = sem("c_z_done"), sem("c_lo_done")
        conv_done, y_done = sem("c_conv_done"), sem("c_y_done")
        stored = [sem(f"c_stored{s}") for s in range(2)]
        agg = sem("c_agg")
        block = c.enter_context(nc.Block())

        @block.sync
        def _(sync):
            sync.dma_start(w_f[:, :, :], w3.rearrange("(t p) m -> p t m", p=P)).then_inc(w_in, 16)

            def body(i, last):
                for s in range(2):
                    sync.wait_ge(y_done, (i * 2 + s + 1) * KT)
                    sync.dma_start(y3_t[:, :, bass.ds((i * 2 + s) * COLS, COLS)], y3s[:, s, :, :])\
                        .then_inc(stored[s], 16)

            over_bodies(sync, body)
            for s in range(2):
                sync.wait_ge(stored[s], BODIES * 16)

        @block.scalar
        def _(act):
            act.wait_ge(sqrt_in, 1)
            nc.scalar.activation(tmp[:, 1, 0:MT], tmp[:, 0, 0:MT], ACT.Sqrt).then_inc(sqrt_out, 1)
            act.wait_ge(bn_done, 1)

            def z(n, s):
                for m in range(MT):
                    src = y[:, m, bass.ds(n * COLS, COLS)]
                    sc, sh = coef[:, m, 0:1], coef[:, m, 1:2]
                    nc.scalar.activation(z_f[:, s, m, :], src, ACT.Relu, bias=sh, scale=sc)
                    nc.scalar.activation(z_hi[:, s, m, :], src, ACT.Relu, bias=sh, scale=sc).then_inc(z_done, 1)

            for s in range(2):
                z(s, s)

            def body(i, first, last):
                for s in range(2):
                    if not first:
                        act.wait_ge(stored[s], i * 16)
                    for m in range(KT):
                        act.wait_ge(conv_done, (i * 2 + s) * KT + m + 1)
                        nc.scalar.activation(y3s[:, s, m, :], ps[:, 4 * s + m % 4, 0:COLS],
                                             ACT.Copy).then_inc(y_done, 1)
                    if not last:
                        z(i * 2 + s + 2, s)

            body(0, True, False)
            with act.Fori(1, BODIES - 1) as i:
                body(i, False, False)
            body(BODIES - 1, False, True)

        @block.vector
        def _(dve):
            step = 0
            for m in range(MT):
                nc.vector.bn_aggr(mv[:, m, :], stats[:, m, :, :].rearrange("p a b -> p (a b)")).then_inc(bn_step, 1)
                step += 1
            dve.wait_ge(bn_step, step)
            step = bn_coefficients(nc, dve, bn_step, step, coef[:, 0:MT, 0], coef[:, 0:MT, 1], mv, tmp,
                                   pv("b2"), pv("g2"), pv("be2"), MT, sqrt_in, sqrt_out)
            nc.vector.memset(tmp[:, 2, 0:1], 0.0).then_inc(bn_done, 1)
            dve.wait_ge(w_in, 16)
            split(nc, dve, w_hi[:, :, :], w_lo[:, :, :], w_f[:, :, :], w_split, 0)

            def lo(n, s):
                dve.wait_ge(z_done, n * 2 + MT)
                nc.vector.tensor_tensor(z_lo[:, s, :, :], z_f[:, s, :, :], z_hi[:, s, :, :].bitcast(F32),
                                        ALU.subtract).then_inc(lo_done, 1)

            for s in range(2):
                lo(s, s)

            def body(i, last):
                for s in range(2):
                    for m in range(KT):
                        dve.wait_ge(y_done, (i * 2 + s) * KT + m + 1)
                        nc.vector.bn_stats(stats3[:, m, bass.ds(i * 2 + s, 1), :].rearrange("p a b -> p (a b)"),
                                           y3s[:, s, m, :])
                    if not last:
                        lo(i * 2 + s + 2, s)

            over_bodies(dve, body)
            nc.vector.memset(tmp[:, 3, 0:1], 0.0).then_inc(bn_step, 1)
            dve.wait_ge(bn_step, step + 1)
            for m in range(KT):
                nc.vector.bn_aggr(mv[:, m, :], stats3[:, m, :, :].rearrange("p a b -> p (a b)")).then_inc(agg, 1)

        @block.tensor
        def _(pe):
            pe.wait_ge(w_split, 2)

            def body(i, last):
                for s in range(2):
                    pe.wait_ge(lo_done, i * 2 + s + 1)
                    for m in range(KT):
                        if m >= 4:
                            pe.wait_ge(y_done, (i * 2 + s) * KT + m - 3)
                        steps = [(w, v, k) for k in range(MT) for w, v in ((w_hi, z_hi), (w_lo, z_hi), (w_hi, z_lo))]
                        for at, (w, v, k) in enumerate(steps):
                            last_mm = nc.tensor.matmul(ps[:, 4 * s + m % 4, 0:COLS], w[:, k, m * P:(m + 1) * P],
                                                       v[:, s, k, :], start=at == 0, stop=at == len(steps) - 1)
                        last_mm.then_inc(conv_done, 1)

            over_bodies(pe, body)


def diagonal(a, c, n, start):
    length, stride = a.shape[1], P - GC
    if c == KT - 1:
        parts = ((0, KT // 2, GC * c), (KT // 2, KT // 2, GC * c + KT // 2 * stride))
    else:
        parts = ((0, KT - 1 - c, P * (c + 1) + stride), (KT - 1 - c, c + 1, GC * c))
    for q, count, row in parts:
        first = a[row:row + 1, bass.ds(start, n)]
        yield q * GC, count * GC, bass.AP(a.tensor, first.offset, [[stride * length, count], [length, GC], [1, n]])


def later(at, d):
    p, i, s = at
    i, s = (i + 1, s) if d == 2 else (i + s, 1 - s)
    if isinstance(i, int) and i == BODIES:
        p, i = p + 1, 0
    return (p, i, s) if p < PASSES else None


def before(at):
    p, i, s = at
    if s:
        return p, i, 0
    if isinstance(i, int) and i == 0:
        return (p - 1, BODIES - 1, 1) if p else None
    return p, i - 1, 1


def over_steps(engine, step):
    for p in range(PASSES):
        for s in range(2):
            step((p, 0, s))
        with engine.Fori(1, BODIES - 1) as i:
            for s in range(2):
                step((p, i, s))
        for s in range(2):
            step((p, BODIES - 1, s))


def layer1(nc, x, x_t, y3, y3_t, out_t, wmain, wside, wout_a, wout_b, mv, tmp, coef, pv, sp):
    coef_dram = nc.dram_tensor("coef_spill", [C_IN, 2], F32).ap()
    with ExitStack() as c:
        sb = lambda name, shape, dt: c.enter_context(nc.sbuf_tensor(name, shape, dt))
        sem = lambda name: c.enter_context(nc.semaphore(name))
        bank = lambda name: c.enter_context(nc.psum_tensor(name, [P, 512], F32))
        coef_sk = sb("d_coef_sk", [P, KT, 2], F32)
        w_raw = sb("d_w_raw", [P, 2, WPP * P], F32)
        w_main_hi, w_main_lo, w_side_hi, w_side_lo, w_out = (
            [sb(f"d_w_{name}{s}", [P, WPP * P], F32R) for s in range(2)]
            for name in ("main_hi", "main_lo", "side_hi", "side_lo", "out"))
        x_win = sb("d_x_win", [P, 2, WT, COLS], F32)
        y_win = sb("d_y_win", [P, 2, WT, COLS], F32)
        x_res = sb("d_x_res", [P, 2, 2, COLS], F32)
        y_res = sb("d_y_res", [P, 2, 2, COLS], F32)
        v_hi = sb("d_v_hi", [P, 2, WT, PAD], F32R)
        v_lo = sb("d_v_lo", [P, 2, WT, PAD], F32R)
        low = sb("d_low", [P, 2, 2, PAD], F32R)
        upp = sb("d_upp", [P, 2, 2, PAD], F32R)
        h_f = sb("d_h", [P, HB, COLS], F32)
        h_hi = sb("d_h_hi", [P, HB, COLS], F32R)
        h_lo = sb("d_h_lo", [P, HB, COLS], F32R)
        part = sb("d_part", [P, 2, COLS], F32)
        res = sb("d_res", [P, 4, COLS], F32)
        hid = [bank(f"d_hid{b}") for b in range(HB)]
        acc = [[bank(f"d_acc{oo}{h}") for h in range(2)] for oo in range(2)]

        raw_in, w_step, pads_done = sem("d_raw_in"), sem("d_w_step"), sem("d_pads_done")
        sk_in, bn_step, sqrt_in, sqrt_out, bn_done = (
            sem(f"d_{n}") for n in ("sk_in", "bn_step", "sqrt_in", "sqrt_out", "bn_done"))
        win_in, res_in, stack_in = ([sem(f"d_{n}_in{s}") for s in range(2)] for n in ("win", "res", "stack"))
        win_sum, win_relu, win_lo = sem("d_win_sum"), sem("d_win_relu"), sem("d_win_lo")
        res_sum, res_relu = sem("d_res_sum"), sem("d_res_relu")
        first_done, h_done, hi_done, lo_done = (
            sem(f"d_{n}") for n in ("first_done", "h_done", "hi_done", "lo_done"))
        oct_done, part_done, comb_done, fin_done = (
            sem(f"d_{n}") for n in ("oct_done", "part_done", "comb_done", "fin_done"))
        stored = [sem(f"d_stored{o}") for o in range(4)]
        block = c.enter_context(nc.Block())

        number = lambda at: at[1] * 2 + (at[0] * PAIRS + at[2])
        pair = lambda at: at[1] * 2 + at[2]
        fills = lambda at: at[1] + (at[0] * BODIES + 1)

        @block.sync
        def _(sync):
            def load_window(at):
                p, _, s = at
                third = (2 * p + 2) % KT
                cols = bass.ds(pair(at) * COLS, COLS)
                for dst, src in ((x_win, x_t), (y_win, y3_t)):
                    sync.dma_start(dst[:, s, 0:2, :], src[:, 2 * p:2 * p + 2, cols]).then_inc(win_in[s], 16)
                    sync.dma_start(dst[:, s, 2, :], src[:, third, cols]).then_inc(win_in[s], 16)

            def load_residual(at):
                p, _, s = at
                for oo in range(2):
                    for dst, src in ((x_res, x), (y_res, y3)):
                        for first, count, pattern in diagonal(src, 2 * p + oo, COLS, pair(at) * COLS):
                            sync.dma_start(dst[first:first + count, s, oo, :], pattern).then_inc(res_in[s], 16)

            def load_stacks(at):
                s = at[2]
                sync.wait_ge(win_lo, (number(at) + 1) * WT)
                for dst, half, t in ((low, 0, 1), (upp, P // 2, 0)):
                    for first, src in ((0, v_hi), (P // 2, v_lo)):
                        sync.dma_start(dst[first:first + P // 2, s, :, :].bitcast(F32),
                                       src[half:half + P // 2, s, t:t + 2, :].bitcast(F32))\
                            .then_inc(stack_in[s], 16)

            def load_raw(p, sources):
                for b, src in enumerate(sources):
                    sync.dma_start(w_raw[:, b, :], src[:, p * WPP * P:(p + 1) * WPP * P]).then_inc(raw_in, 16)

            def store(at, oo):
                o = 2 * at[2] + oo
                sync.wait_ge(fin_done, number(at) * 2 + oo + 1)
                sync.dma_start(out_t[:, 2 * at[0] + oo, bass.ds(pair(at) * COLS, COLS)], res[:, o, :])\
                    .then_inc(stored[o], 16)

            load_window((0, 0, 0))
            load_raw(0, (wmain, wside))
            load_window((0, 0, 1))
            load_residual((0, 0, 0))
            sync.wait_ge(bn_done, 1)
            sync.dma_start(coef_dram.rearrange("(t p) a -> p t a", p=P), coef[:, :, :]).then_inc(stored[3], 16)
            sync.wait_ge(stored[3], 16)
            for tile in range(KT):
                for first, count, pattern in diagonal(coef_dram, tile, 2, 0):
                    sync.dma_start(coef_sk[first:first + count, tile, :], pattern).then_inc(sk_in, 16)
            sync.wait_ge(w_step, 4)
            load_raw(0, (wout_a, wout_b))
            load_stacks((0, 0, 0))

            def step(at):
                p, i, s = at
                if (then := later(at, 2)) is not None:
                    sync.wait_ge(win_lo, (number(at) + 1) * WT)
                    load_window(then)
                if (prev := before(at)) is not None:
                    store(prev, 1)
                if (then := later(at, 1)) is not None:
                    load_residual(then)
                    load_stacks(then)
                store(at, 0)
                if isinstance(i, int) and p + 1 < PASSES:
                    if (i, s) == (0, 0):
                        sync.wait_ge(w_step, 8 * (p + 1))
                        load_raw(p + 1, (wmain, wside))
                    if (i, s) == (0, 1):
                        sync.wait_ge(w_step, 8 * (p + 1) + 4)
                        load_raw(p + 1, (wout_a, wout_b))

            over_steps(sync, step)
            store((PASSES - 1, BODIES - 1, 1), 1)
            for o in range(4):
                sync.wait_ge(stored[o], 16 * (PASSES * BODIES + (o == 3)))

        @block.gpsimd
        def _(pool):
            nc.gpsimd.memset(v_hi[:, :, :, :].bitcast(F32), 0.0).then_inc(pads_done, 1)
            nc.gpsimd.memset(v_lo[:, :, :, :].bitcast(F32), 0.0).then_inc(pads_done, 1)
            with pool.Fori(0, PASSES * BODIES) as b:
                for o in range(4):
                    pool.wait_ge(comb_done, b * 4 + o + 1)
                    pool.wait_ge(res_relu, b * 4 + o + 1)
                    nc.gpsimd.tensor_tensor(res[:, o, :], res[:, o, :], x_res[:, o // 2, o % 2, :],
                                            ALU.add).then_inc(fin_done, 1)

        @block.scalar
        def _(act):
            act.wait_ge(sqrt_in, 1)
            nc.scalar.activation(tmp[:, 1, :], tmp[:, 0, :], ACT.Sqrt).then_inc(sqrt_out, 1)
            act.wait_ge(bn_done, 1)
            act.wait_ge(pads_done, 2)

            def window_tile(at, t):
                p, _, s = at
                shift = coef[:, (2 * p + t) % KT, 1:2]
                act.wait_ge(win_sum, number(at) * WT + t + 1)
                nc.scalar.activation(inner(v_hi[:, s, t, :]), rows(y_win[:, s, t, :]), ACT.Relu, bias=shift)
                nc.scalar.activation(x_win[:, s, t, :], y_win[:, s, t, :], ACT.Relu, bias=shift).then_inc(win_relu, 1)

            def residual_tile(at, oo):
                p, _, s = at
                act.wait_ge(res_sum, number(at) * 2 + oo + 1)
                nc.scalar.activation(x_res[:, s, oo, :], y_res[:, s, oo, :], ACT.Relu,
                                     bias=coef_sk[:, 2 * p + oo, 1:2]).then_inc(res_relu, 1)

            def move_low_parts(at, oo):
                act.wait_ge(oct_done, number(at) * 2 + oo + 1)
                nc.scalar.activation(part[P // 2:P, oo, :], acc[oo][0][0:P // 2, 0:COLS], ACT.Copy)
                nc.scalar.activation(part[0:P // 2, oo, :], acc[oo][1][P // 2:P, 0:COLS], ACT.Copy)\
                    .then_inc(part_done, 1)

            for t in range(WT):
                window_tile((0, 0, 0), t)

            def step(at):
                p = at[0]
                hb = pv("hid_b")
                for g in range(WPP):
                    act.wait_ge(first_done, number(at) * WPP + g + 1)
                    k = p * WPP + g
                    nc.scalar.activation(h_f[:, g % HB, :], hid[g % HB][:, 0:COLS], ACT.Relu,
                                         bias=hb[:, k:k + 1]).then_inc(h_done, 1)
                    if g in (1, 3, 5) and (then := later(at, 1)) is not None:
                        window_tile(then, g // 2)
                    if g in (9, 10):
                        residual_tile(at, g - 9)
                    if g == 3 and (prev := before(at)) is not None:
                        move_low_parts(prev, 1)
                    if g == 11:
                        move_low_parts(at, 0)

            over_steps(act, step)
            move_low_parts((PASSES - 1, BODIES - 1, 1), 1)

        @block.vector
        def _(dve):
            bn_coefficients(nc, dve, bn_step, 0, coef[:, :, 0], coef[:, :, 1], mv, tmp, pv("b3"), pv("g3"),
                            pv("be3"), KT, sqrt_in, sqrt_out, by=sp[:, 0:1])
            nc.vector.memset(sp[:, 7:8], 0.0).then_inc(bn_done, 1)
            dve.wait_ge(pads_done, 2)

            def window_sum(at, t):
                p, _, s = at
                dve.wait_ge(win_in[s], fills(at) * 64)
                nc.vector.scalar_tensor_tensor(y_win[:, s, t, :], y_win[:, s, t, :], coef[:, (2 * p + t) % KT, 0:1],
                                               x_win[:, s, t, :], op0=ALU.mult, op1=ALU.add).then_inc(win_sum, 1)

            def window_lo(at, t):
                s = at[2]
                dve.wait_ge(win_relu, number(at) * WT + t + 1)
                nc.vector.tensor_tensor(inner(v_lo[:, s, t, :]), rows(x_win[:, s, t, :]),
                                        inner(v_hi[:, s, t, :]).bitcast(F32), ALU.subtract).then_inc(win_lo, 1)

            def residual_sum(at, oo):
                p, _, s = at
                dve.wait_ge(res_in[s], fills(at) * 128)
                nc.vector.scalar_tensor_tensor(y_res[:, s, oo, :], y_res[:, s, oo, :],
                                               coef_sk[:, 2 * p + oo, 0:1], x_res[:, s, oo, :],
                                               op0=ALU.mult, op1=ALU.add).then_inc(res_sum, 1)

            def combine(at, oo):
                p, _, s = at
                o = 2 * s + oo
                dve.wait_ge(part_done, number(at) * 2 + oo + 1)
                if o == 3:
                    dve.wait_ge(stored[o], fills(at) * 16)
                elif not (isinstance(at[1], int) and p == at[1] == 0):
                    dve.wait_ge(stored[o], fills(at) * 16 - 16)
                for half, h in ((slice(P // 2, P), 0), (slice(0, P // 2), 1)):
                    ins = nc.vector.scalar_tensor_tensor(
                        res[half, o, :], acc[oo][h][half, 0:COLS], pv("out_b")[half, 2 * p + oo:2 * p + oo + 1],
                        part[half, oo, :], op0=ALU.add, op1=ALU.add)
                ins.then_inc(comb_done, 1)

            def weights(p, i):
                b = p % 2
                if i:
                    dve.wait_ge(w_step, 8 * p + i)
                if i in (0, 4):
                    dve.wait_ge(raw_in, 64 * p + 32 + 8 * i)
                if i < 4:
                    hi, lo = ((w_main_hi, w_main_lo), (w_side_hi, w_side_lo))[i // 2]
                    if i % 2 == 0:
                        ins = nc.vector.tensor_copy(hi[b][:, :], w_raw[:, i // 2, :])
                    else:
                        ins = nc.vector.tensor_tensor(lo[b][:, :], w_raw[:, i // 2, :], hi[b][:, :].bitcast(F32),
                                                      ALU.subtract)
                elif i == 4:
                    ins = nc.vector.tensor_copy(w_out[b][:, :], w_raw[:, 1, :])
                elif i == 5:
                    ins = nc.vector.tensor_tensor(w_raw[:, 1, :], w_raw[:, 1, :], w_out[b][:, :].bitcast(F32),
                                                  ALU.subtract)
                elif i == 6:
                    ins = nc.vector.tensor_copy(w_out[b][:, :], w_raw[:, 0, :])
                else:
                    ins = nc.vector.tensor_tensor(w_out[b][:, :], w_out[b][:, :].bitcast(F32), w_raw[:, 1, :], ALU.add)
                ins.then_inc(w_step, 1)

            for t in range(WT):
                window_sum((0, 0, 0), t)
            for i in range(4):
                weights(0, i)
            for t in range(WT):
                window_lo((0, 0, 0), t)
            for i in range(4, 8):
                weights(0, i)
            dve.wait_ge(sk_in, 2 * KT * 16)

            def hidden_lo(count, b):
                dve.wait_ge(hi_done, count)
                nc.vector.tensor_tensor(h_lo[:, b, :], h_f[:, b, :], h_hi[:, b, :].bitcast(F32),
                                        ALU.subtract).then_inc(lo_done, 1)

            def step(at):
                p, i, s = at
                for g in range(WPP):
                    G = number(at) * WPP + g
                    dve.wait_ge(h_done, G + 1)
                    nc.vector.tensor_copy(h_hi[:, g % HB, :], h_f[:, g % HB, :]).then_inc(hi_done, 1)
                    if g or before(at) is not None:
                        hidden_lo(G, (g - 1) % HB)
                    if (then := later(at, 1)) is not None:
                        if g in (0, 2, 4):
                            window_sum(then, g // 2)
                        if g in (4, 6, 8):
                            window_lo(then, g // 2 - 2)
                    if g in (9, 10):
                        residual_sum(at, g - 9)
                    if g == 3 and (prev := before(at)) is not None:
                        combine(prev, 1)
                    if g == 11:
                        combine(at, 0)
                    if isinstance(i, int) and p + 1 < PASSES and g in (7, 12, 13, 15):
                        at_w = (7, 12, 13, 15).index(g)
                        if (i, s) == (0, 1):
                            weights(p + 1, at_w)
                        if (i, s) == (BODIES - 1, 0):
                            weights(p + 1, 4 + at_w)

            over_steps(dve, step)
            hidden_lo(PASSES * PAIRS * WPP, HB - 1)
            combine((PASSES - 1, BODIES - 1, 1), 1)

        @block.tensor
        def _(pe):
            def first_product(at, g):
                p, i, s = at
                b, k = p % 2, p * WPP + g
                oo, j = divmod(g, OCT)
                if g == 0:
                    if isinstance(i, int) and (i, s) == (0, 0):
                        pe.wait_ge(w_step, 8 * (p + 1))
                    pe.wait_ge(win_lo, (number(at) + 1) * WT)
                    pe.wait_ge(stack_in[s], fills(at) * 64)
                if j < OCT // 2:
                    main, side, main_tile, side_tile = oo, low, 0, 1
                else:
                    main, side, main_tile, side_tile = oo + 1, upp, 1, 0
                cols = slice(g * P, (g + 1) * P)
                at_main, at_side = (SHIFTS[shift_of(k, t)] for t in (main_tile, side_tile))
                products = ((w_main_hi, v_hi[:, s, main, :], at_main), (w_main_lo, v_hi[:, s, main, :], at_main),
                            (w_main_hi, v_lo[:, s, main, :], at_main), (w_side_hi, side[:, s, oo, :], at_side),
                            (w_side_lo, side[:, s, oo, :], at_side))
                for n, (w, v, shift) in enumerate(products):
                    ins = nc.tensor.matmul(hid[g % HB][:, 0:COLS], w[b][:, cols], inner(v, *shift),
                                           start=n == 0, stop=n == len(products) - 1)
                ins.then_inc(first_done, 1)

            def second_product(at, g):
                p = at[0]
                oo, j = divmod(g, OCT)
                pe.wait_ge(lo_done, number(at) * WPP + g + 1)
                h, q = divmod(j, OCT // 2)
                for n, v in enumerate((h_hi, h_lo)):
                    ins = nc.tensor.matmul(acc[oo][h][:, 0:COLS], w_out[p % 2][:, g * P:(g + 1) * P], v[:, g % HB, :],
                                           start=q == n == 0, stop=q == OCT // 2 - 1 and n == 1)
                if j == OCT - 1:
                    ins.then_inc(oct_done, 1)

            for g in range(LAG):
                first_product((0, 0, 0), g)

            def step(at):
                for g in range(WPP):
                    if g + LAG < WPP:
                        first_product(at, g + LAG)
                    elif (then := later(at, 1)) is not None:
                        first_product(then, g + LAG - WPP)
                    second_product(at, g)

            over_steps(pe, step)


def window_weights(w1, w2, b2):
    main, side, out_a, out_b = (np.zeros((GROUPS, P, P), w1.dtype) for _ in range(4))
    bias = np.zeros((P, KT), b2.dtype)
    for k in range(GROUPS):
        m, (c, j) = group_of(k), divmod(k, OCT)
        w, cut = w1[m].T, P - GC * j
        if j < OCT // 2:
            main[k, GC * j:] = w[:cut]
            half, first = w[cut:], 0
        else:
            main[k, :GC * (j + 1)] = w[cut:]
            half, first = w[:cut], GC * j - P // 2
        for stack in (0, P // 2):
            side[k, stack + first:stack + first + len(half)] = half
        q = GC * (OCT - 1 - j)
        out_a[k, :, q:q + GC] = w2[m].T
        out_b[k, :, (q + P // 2) % P:(q + P // 2) % P + GC] = w2[m].T
        bias[q:q + GC, c] = b2[GC * m:GC * (m + 1)]
    by_row = lambda a: np.ascontiguousarray(a.transpose(1, 0, 2)).reshape(P, GROUPS * P)
    return by_row(main), by_row(side), by_row(out_a), by_row(out_b), bias


def kernel(x, L0_conv_w1, L0_conv_b1, L0_conv_g1, L0_conv_be1, L0_conv_w2, L0_conv_b2, L0_conv_g2, L0_conv_be2,
           L0_conv_w3, L0_conv_b3, L0_conv_g3, L0_conv_be3, L0_conv_residual_scale, L1_conv_w1, L1_conv_b1,
           L1_conv_w2, L1_conv_b2):
    import concourse.bacc as bacc
    from concourse.bass_utils import run_bass_kernel_spmd

    wmain, wside, wout_a, wout_b, out_b = window_weights(np.asarray(L1_conv_w1), np.asarray(L1_conv_w2),
                                                         np.asarray(L1_conv_b2))
    by_tile = lambda a: np.asarray(a).reshape(-1, P).T
    hid_b = np.asarray(L1_conv_b1).reshape(GROUPS, HID)[[group_of(k) for k in range(GROUPS)]].T
    vectors = [by_tile(a) for a in (L0_conv_b1, L0_conv_g1, L0_conv_be1, L0_conv_b2, L0_conv_g2, L0_conv_be2,
                                    L0_conv_b3, L0_conv_g3, L0_conv_be3)]
    vectors += [np.repeat(np.asarray(L0_conv_residual_scale).reshape(1, 1), P, 0), hid_b, out_b]
    arrays = {
        "x": np.asarray(x).transpose(1, 0, 2, 3).reshape(C_IN, T),
        "w1": np.asarray(L0_conv_w1).reshape(C_MID, C_IN).T,
        "w2": np.asarray(L0_conv_w2).reshape(C_MID, C_MID, 9).transpose(1, 2, 0),
        "w3": np.asarray(L0_conv_w3).reshape(C_IN, C_MID).T,
        "wmain": wmain, "wside": wside, "wout_a": wout_a, "wout_b": wout_b,
        "params": np.concatenate(vectors, axis=1),
    }
    arrays = {f"{name}_dram": np.ascontiguousarray(a) for name, a in arrays.items()}
    nc = bacc.Bacc("TRN2", target_bir_lowering=False, num_devices=1)
    args = [nc.dram_tensor(name, a.shape, mybir.dt.from_np(a.dtype), kind="ExternalInput").ap()
            for name, a in arrays.items()]
    out = nc.dram_tensor("out_dram", [C_IN, T], F32, kind="ExternalOutput").ap()
    build(nc, *args, out)
    got = run_bass_kernel_spmd(nc, [arrays], core_ids=[0]).results[0]["out_dram"]
    got = np.asarray(got).reshape(KT, OCT, GC, N_IMG, H, W)
    result = np.empty((KT, OCT, GC, N_IMG, H, W), got.dtype)
    for c in range(KT):
        for q in range(OCT):
            result[(c - OCT + 1 + q) % KT, OCT - 1 - q] = got[c, q]
    return np.ascontiguousarray(result.reshape(C_IN, N_IMG, H, W).transpose(1, 0, 2, 3))
```

```python
from contextlib import ExitStack

import numpy as np

import concourse.bass as bass
from concourse import mybir

F32 = mybir.dt.float32
F32R = mybir.dt.float32r
ACT = mybir.ActivationFunctionType
ALU = mybir.AluOpType

P = 128
N_IMG, C_IN, H, W = 64, 1024, 14, 14
C_MID = 256
PAIRS = N_IMG // 2
COLS = 2 * H * W
T = N_IMG * H * W
PAD = 2 * (H + 2) * (W + 2)
KT = C_IN // P
MT = C_MID // P
BODIES = PAIRS // 2
TAPS = [(r, c) for r in (-1, 0, 1) for c in (-1, 0, 1)]
BN_EPS = 1e-5

GROUPS, GC, HID = 64, 16, 128
SHIFTS = [(0, 0)] + [t for t in TAPS if t != (0, 0)]
PASSES = 4
WPP = GROUPS // PASSES
WT = 3
OCT = 8
LAG = 6
BANKS = 4
HB = 8
QUARTER = P // 4
W_STAGES = (0, 2, 6, 10, 14)
W_STEPS = W_STAGES[-1]


def group_of(k):
    return pow(9, -1, GROUPS) * k % GROUPS


def shift_of(k, tile):
    s = (9 * group_of(k) * GC) // C_IN
    return s + 1 if tile and k // OCT + 1 == KT else s


PARAMS = {}
_at = 0
for _name, _n in (("b1", MT), ("g1", MT), ("be1", MT), ("b2", MT), ("g2", MT), ("be2", MT),
                  ("b3", KT), ("g3", KT), ("be3", KT), ("rs", 1), ("hid_b", GROUPS), ("out_b", KT)):
    PARAMS[_name] = (_at, _at + _n)
    _at += _n
N_PARAMS = _at


def build(nc, x, w1, w2, w3, wmain, wside, wout_a, wout_b, params, out):
    y3 = nc.dram_tensor("y3_spill", [C_IN, T], F32).ap()
    x_t = x.rearrange("(t p) n -> p t n", p=P)
    y3_t = y3.rearrange("(t p) n -> p t n", p=P)
    out_t = out.rearrange("(t p) n -> p t n", p=P)

    with ExitStack() as ctx:
        par = ctx.enter_context(nc.sbuf_tensor("par", [P, N_PARAMS], F32))
        coef = ctx.enter_context(nc.sbuf_tensor("coef", [P, KT, 2], F32))
        mv = ctx.enter_context(nc.sbuf_tensor("mv", [P, KT, 2], F32))
        tmp = ctx.enter_context(nc.sbuf_tensor("tmp", [P, 4, KT], F32))
        sp = ctx.enter_context(nc.sbuf_tensor("sp", [P, 8], F32))
        par_in = ctx.enter_context(nc.semaphore("par_in"))

        def pv(name):
            a, b = PARAMS[name]
            return par[:, a:b]

        with ExitStack() as mid:
            y = mid.enter_context(nc.sbuf_tensor("y", [P, MT, T], F32))
            stats = mid.enter_context(nc.sbuf_tensor("stats", [P, MT, PAIRS, 6], F32))
            conv1(nc, x_t, w1, y, stats, par, params, par_in, pv, sp)
            conv2(nc, w2, y, stats, mv, tmp, coef, pv)
            conv3(nc, w3, y, stats, mv, tmp, coef, pv, y3_t)
        layer1(nc, x, x_t, y3, y3_t, out_t, wmain, wside, wout_a, wout_b, mv, tmp, coef, pv, sp)


def split(nc, dve, hi, lo, v, done, count):
    nc.vector.tensor_copy(hi, v).then_inc(done, 1)
    dve.wait_ge(done, count + 1)
    nc.vector.tensor_tensor(lo, v, hi.bitcast(F32), ALU.subtract).then_inc(done, 1)
    return count + 2


def bn_coefficients(nc, dve, step, count, scale, shift, mv, tmp, b, g, be, n, sqrt_in, sqrt_out, by=None):
    def then(ins):
        nonlocal count
        count += 1
        ins.then_inc(step, 1)
        dve.wait_ge(step, count)

    mean, var = mv[:, 0:n, 0], mv[:, 0:n, 1]
    v, r, e, m = (tmp[:, i, 0:n] for i in range(4))
    then(nc.vector.tensor_tensor(m, mean, b, ALU.add))
    nc.vector.tensor_scalar(v, var, BN_EPS, None, ALU.add).then_inc(sqrt_in, 1)
    dve.wait_ge(sqrt_out, 1)
    then(nc.vector.reciprocal(r, r))
    then(nc.vector.tensor_tensor(e, v, r, ALU.mult))
    then(nc.vector.tensor_tensor(e, e, r, ALU.mult))
    then(nc.vector.tensor_scalar(e, e, -0.5, 1.5, ALU.mult, ALU.add))
    then(nc.vector.tensor_tensor(r, r, e, ALU.mult))
    then(nc.vector.tensor_tensor(scale, r, g, ALU.mult))
    then(nc.vector.tensor_tensor(m, b, m, ALU.subtract))
    then(nc.vector.tensor_tensor(m, m, scale, ALU.mult))
    then(nc.vector.tensor_tensor(shift, m, be, ALU.add))
    if by is not None:
        then(nc.vector.tensor_scalar(scale, scale, by, None, ALU.mult))
        then(nc.vector.tensor_scalar(shift, shift, by, None, ALU.mult))
    return count


def over_bodies(engine, body):
    with engine.Fori(0, BODIES - 1) as i:
        body(i, False)
    body(BODIES - 1, True)


def conv1(nc, x_t, w1, y, stats, par, params, par_in, pv, sp):
    with ExitStack() as c:
        sb = lambda name, shape, dt: c.enter_context(nc.sbuf_tensor(name, shape, dt))
        sem = lambda name: c.enter_context(nc.semaphore(name))
        w_f = sb("a_w", [P, KT, C_MID], F32)
        w_hi = sb("a_w_hi", [P, KT, C_MID], F32R)
        w_lo = sb("a_w_lo", [P, KT, C_MID], F32R)
        x_f = sb("a_x", [P, 2, KT, COLS], F32)
        x_hi = sb("a_x_hi", [P, 2, KT, COLS], F32R)
        x_lo = sb("a_x_lo", [P, 2, KT, COLS], F32R)
        ps = c.enter_context(nc.psum_tensor("a_ps", [P, 4, 512], F32))
        w_in = sem("a_w_in")
        w_split = sem("a_w_split")
        x_in = [sem(f"a_x_in{s}") for s in range(2)]
        hi_done, lo_done = sem("a_hi_done"), sem("a_lo_done")
        conv_done, y_done = sem("a_conv_done"), sem("a_y_done")
        sp_step, sp_exp, sp_ln = sem("a_sp_step"), sem("a_sp_exp"), sem("a_sp_ln")
        block = c.enter_context(nc.Block())

        @block.sync
        def _(sync):
            sync.dma_start(w_f[:, :, :], w1.rearrange("(t p) m -> p t m", p=P)).then_inc(w_in, 16)

            def load(n, s):
                sync.dma_start(x_f[:, s, :, :], x_t[:, :, bass.ds(n * COLS, COLS)]).then_inc(x_in[s], 16)

            for s in range(2):
                load(s, s)
            sync.dma_start(par[:, :], params).then_inc(par_in, 16)

            def body(i, last):
                for s in range(2):
                    if not last:
                        sync.wait_ge(lo_done, i * 2 + s + 1)
                        load(i * 2 + s + 2, s)

            over_bodies(sync, body)
            sync.wait_ge(par_in, 16)

        @block.scalar
        def _(act):
            def hi(s, uses):
                act.wait_ge(x_in[s], uses * 16)
                nc.scalar.activation(x_hi[:, s, :, :], x_f[:, s, :, :], ACT.Copy).then_inc(hi_done, 1)

            for s in range(2):
                hi(s, 1)
            softplus_act(nc, act, sp, sp_step, sp_exp, sp_ln)

            def body(i, last):
                for s in range(2):
                    for m in range(MT):
                        act.wait_ge(conv_done, i * 4 + 2 * s + m + 1)
                        nc.scalar.activation(y[:, m, bass.ds((i * 2 + s) * COLS, COLS)], ps[:, 2 * s + m, 0:COLS],
                                             ACT.Copy).then_inc(y_done, 1)
                    if not last:
                        hi(s, i + 2)

            over_bodies(act, body)

        @block.vector
        def _(dve):
            dve.wait_ge(w_in, 16)
            split(nc, dve, w_hi[:, :, :], w_lo[:, :, :], w_f[:, :, :], w_split, 0)

            def lo(s, n):
                dve.wait_ge(hi_done, n + 1)
                nc.vector.tensor_tensor(x_lo[:, s, :, :], x_f[:, s, :, :], x_hi[:, s, :, :].bitcast(F32),
                                        ALU.subtract).then_inc(lo_done, 1)

            for s in range(2):
                lo(s, s)
            dve.wait_ge(par_in, 16)
            softplus_dve(nc, dve, sp, pv("rs"), sp_step, sp_exp, sp_ln)

            def body(i, last):
                for s in range(2):
                    for m in range(MT):
                        dve.wait_ge(y_done, i * 4 + 2 * s + m + 1)
                        nc.vector.bn_stats(stats[:, m, bass.ds(i * 2 + s, 1), :].rearrange("p a b -> p (a b)"),
                                           y[:, m, bass.ds((i * 2 + s) * COLS, COLS)])
                    if not last:
                        lo(s, i * 2 + s + 2)

            over_bodies(dve, body)

        @block.tensor
        def _(pe):
            pe.wait_ge(w_split, 2)

            def body(i, last):
                for s in range(2):
                    pe.wait_ge(lo_done, i * 2 + s + 1)
                    for m in range(MT):
                        steps = [(w, v, k) for k in range(KT) for w, v in ((w_hi, x_hi), (w_lo, x_hi), (w_hi, x_lo))]
                        for at, (w, v, k) in enumerate(steps):
                            last_mm = nc.tensor.matmul(ps[:, 2 * s + m, 0:COLS], w[:, k, m * P:(m + 1) * P],
                                                       v[:, s, k, :], start=at == 0, stop=at == len(steps) - 1)
                        last_mm.then_inc(conv_done, 1)

            over_bodies(pe, body)


def conv2(nc, w2, y, stats, mv, tmp, coef, pv):
    rows4 = 4 * (H // 2)
    v_cols = rows4 * (W + 2)
    units = N_IMG // 4
    with ExitStack() as c:
        sb = lambda name, shape, dt: c.enter_context(nc.sbuf_tensor(name, shape, dt))
        sem = lambda name: c.enter_context(nc.semaphore(name))
        w_hi = sb("b_w_hi", [P, MT, 4, 3, C_MID], F32R)
        w_lo = sb("b_w_lo", [P, MT, 4, 3, C_MID], F32R)
        w_f0 = sb("b_w_f0", [P, 3, 3, C_MID], F32)
        spare = sb("b_spare", [P, 6 * COLS], F32)
        w_f = (w_f0[:, :, :, :], spare[:, 0:9 * C_MID].rearrange("p (a b m) -> p a b m", a=3, b=3))
        m2_f, t1, t2 = (spare[:, n * MT * COLS:(n + 1) * MT * COLS].rearrange("p (m n) -> p m n", m=MT)
                        for n in range(3))
        z = sb("b_z", [P, MT * 4 * (H + 2) * (W + 2)], F32)
        v_f = sb("b_v", [P, MT, v_cols], F32)
        v_hi = sb("b_v_hi", [P, 4, MT, v_cols], F32R)
        v_lo = sb("b_v_lo", [P, 4, MT, v_cols], F32R)
        bank = [[c.enter_context(nc.psum_tensor(f"b_m{f}{m}", [P, 512], F32)) for m in range(MT)] for f in range(4)]
        w_in = [sem(f"b_w_in{k}") for k in range(MT)]
        w_step, pads_done = sem("b_w_step"), sem("b_pads_done")
        bn_step, sqrt_in, sqrt_out, bn_done = sem("b_bn_step"), sem("b_sqrt_in"), sem("b_sqrt_out"), sem("b_bn_done")
        z_done, v_done, hi_done, lo_done = sem("b_z_done"), sem("b_v_done"), sem("b_hi_done"), sem("b_lo_done")
        mm_done, m2_done, t_done = sem("b_mm_done"), sem("b_m2_done"), sem("b_t_done")
        even_done, odd_done = sem("b_even_done"), sem("b_odd_done")
        block = c.enter_context(nc.Block())

        def over_units(engine, unit):
            unit(0, False)
            with engine.Fori(1, units - 1) as u:
                unit(u, False)
            unit(units - 1, True)

        @block.sync
        def _(sync):
            w2_t = w2.rearrange("(t p) (a b) m -> p t a b m", p=P, a=3)
            for k in range(MT):
                sync.dma_start(w_f[k], w2_t[:, k, :, :, :]).then_inc(w_in[k], 16)
            for k in range(MT):
                sync.wait_ge(w_in[k], 16)

        @block.gpsimd
        def _(pool):
            nc.gpsimd.memset(z[:, :], 0.0).then_inc(pads_done, 1)
            z_rows = z[:, :].rearrange("p (i h w) -> p i h w", h=H + 2, w=W + 2)
            row = lambda a: z_rows[:, :, a:a + H - 1:2, :]
            v_rows = v_f[:, :, :].rearrange("p k (i h w) -> p (k i) h w", i=4, w=W + 2)

            def transform(u):
                pool.wait_ge(z_done, u + 1)
                for f, (a, b, op) in enumerate(((0, 2, ALU.subtract), (1, 2, ALU.add), (2, 1, ALU.subtract),
                                                (1, 3, ALU.subtract))):
                    if f or not (isinstance(u, int) and u == 0):
                        pool.wait_ge(lo_done, u * 4 + f)
                    nc.gpsimd.tensor_tensor(v_rows, row(a), row(b), op).then_inc(v_done, 1)

            transform(0)
            with pool.Fori(1, units) as u:
                transform(u)

        @block.scalar
        def _(act):
            act.wait_ge(sqrt_in, 1)
            nc.scalar.activation(tmp[:, 1, 0:MT], tmp[:, 0, 0:MT], ACT.Sqrt).then_inc(sqrt_out, 1)
            act.wait_ge(bn_done, 1)
            act.wait_ge(pads_done, 1)

            def relu(u):
                for k in range(MT):
                    src = y[:, k, bass.ds(u * 2 * COLS, 2 * COLS)].rearrange("p (i h w) -> p i h w", h=H, w=W)
                    dst = z[:, :].rearrange("p (k i h w) -> p k i h w", k=MT, h=H + 2, w=W + 2)
                    ins = nc.scalar.activation(dst[:, k, :, 1:1 + H, 1:1 + W], src, ACT.Relu, bias=coef[:, k, 1:2],
                                               scale=coef[:, k, 0:1])
                ins.then_inc(z_done, 1)

            def hi(u, f):
                act.wait_ge(v_done, u * 4 + f + 1)
                nc.scalar.activation(v_hi[:, f, :, :], v_f[:, :, :], ACT.Copy).then_inc(hi_done, 1)

            relu(0)
            for f in range(4):
                hi(0, f)

            def unit(u, last):
                if not last:
                    act.wait_ge(v_done, u * 4 + 4)
                    relu(u + 1)
                for f in range(4):
                    act.wait_ge(mm_done, u * 4 + f + 1)
                    if f == 2:
                        for m in range(MT):
                            nc.scalar.activation(m2_f[:, m, :], bank[2][m][:, 0:COLS], ACT.Copy).then_inc(m2_done, 1)
                    if not last:
                        hi(u + 1, f)

            over_units(act, unit)

        @block.vector
        def _(dve):
            step = 0
            for m in range(MT):
                nc.vector.bn_aggr(mv[:, m, :], stats[:, m, :, :].rearrange("p a b -> p (a b)")).then_inc(bn_step, 1)
                step += 1
            dve.wait_ge(bn_step, step)
            bn_coefficients(nc, dve, bn_step, step, coef[:, 0:MT, 0], coef[:, 0:MT, 1], mv, tmp,
                            pv("b1"), pv("g1"), pv("be1"), MT, sqrt_in, sqrt_out)
            nc.vector.memset(tmp[:, 2, 0:1], 0.0).then_inc(bn_done, 1)

            def lo(u, f):
                dve.wait_ge(hi_done, u * 4 + f + 1)
                nc.vector.tensor_tensor(v_lo[:, f, :, :], v_f[:, :, :], v_hi[:, f, :, :].bitcast(F32),
                                        ALU.subtract).then_inc(lo_done, 1)

            count = 0

            def then(ins):
                nonlocal count
                count += 1
                ins.then_inc(w_step, 1)
                dve.wait_ge(w_step, count)

            def split_w(f, k, g):
                then(nc.vector.tensor_copy(w_hi[:, k, f, :, :], w_f[k][:, g, :, :]))
                then(nc.vector.tensor_tensor(w_lo[:, k, f, :, :], w_f[k][:, g, :, :],
                                             w_hi[:, k, f, :, :].bitcast(F32), ALU.subtract))

            for k in range(MT):
                dve.wait_ge(w_in[k], 16)
                split_w(0, k, 0)
            lo(0, 0)
            for k in range(MT):
                g0, g1, g2 = (w_f[k][:, g, :, :] for g in range(3))
                split_w(3, k, 2)
                then(nc.vector.tensor_tensor(g0, g0, g2, ALU.add))
                then(nc.vector.tensor_scalar(g0, g0, 0.5, None, ALU.mult))
                then(nc.vector.scalar_tensor_tensor(g2, g1, 0.5, g0, op0=ALU.mult, op1=ALU.add))
                then(nc.vector.scalar_tensor_tensor(g0, g1, -0.5, g0, op0=ALU.mult, op1=ALU.add))
                split_w(1, k, 2)
                lo(0, 1 + k)
            for k in range(MT):
                split_w(2, k, 0)
            lo(0, 3)

            def unit(u, last):
                out_rows = [y[:, m, bass.ds(u * 2 * COLS, 2 * COLS)].rearrange("p (r e w) -> p r e w", e=2, w=W)
                            for m in range(MT)]
                as_rows = lambda a: a.rearrange("p (r w) -> p r w", w=W)
                for f in range(4):
                    if f == 2:
                        for m in range(MT):
                            dve.wait_ge(m2_done, u * 2 + m + 1)
                            m1 = bank[1][m][:, 0:COLS]
                            nc.vector.tensor_tensor(t1[:, m, :], m1, m2_f[:, m, :], ALU.add).then_inc(t_done, 1)
                            nc.vector.tensor_tensor(t2[:, m, :], m1, m2_f[:, m, :], ALU.subtract).then_inc(t_done, 1)
                        for m in range(MT):
                            dve.wait_ge(t_done, u * 4 + 2 * m + 1)
                            nc.vector.tensor_tensor(out_rows[m][:, :, 0, :], as_rows(bank[0][m][:, 0:COLS]),
                                                    as_rows(t1[:, m, :]), ALU.add).then_inc(even_done, 1)
                    if f == 3:
                        dve.wait_ge(mm_done, u * 4 + 4)
                        dve.wait_ge(t_done, u * 4 + 4)
                        for m in range(MT):
                            nc.vector.tensor_tensor(out_rows[m][:, :, 1, :], as_rows(t2[:, m, :]),
                                                    as_rows(bank[3][m][:, 0:COLS]), ALU.subtract)\
                                .then_inc(odd_done, 1)
                    if not last:
                        lo(u + 1, f)
                for m in range(MT):
                    dve.wait_ge(odd_done, u * 2 + m + 1)
                    for e in range(2):
                        nc.vector.bn_stats(stats[:, m, bass.ds(u * 2 + e, 1), :].rearrange("p a b -> p (a b)"),
                                           y[:, m, bass.ds((u * 2 + e) * COLS, COLS)])

            over_units(dve, unit)

        @block.tensor
        def _(pe):
            ready = (2 * MT, 4 * MT + 8 * MT - 2 * MT, 12 * MT, 12 * MT)

            def unit(u, last):
                for f in range(4):
                    if isinstance(u, int) and u == 0:
                        pe.wait_ge(w_step, ready[f])
                    elif f == 0:
                        pe.wait_ge(even_done, u * 2)
                    pe.wait_ge(lo_done, u * 4 + f + 1)
                    for m in range(MT):
                        steps = [(w, v, k, b) for k in range(MT) for b in range(3)
                                 for w, v in ((w_hi, v_hi), (w_lo, v_hi), (w_hi, v_lo))]
                        for at, (w, v, k, b) in enumerate(steps):
                            rhs = v[:, f, k, :].rearrange("p (r w) -> p r w", w=W + 2)[:, :, b:b + W]
                            ins = nc.tensor.matmul(bank[f][m][:, 0:COLS], w[:, k, f, b, m * P:(m + 1) * P], rhs,
                                                   start=at == 0, stop=at == len(steps) - 1)
                    ins.then_inc(mm_done, 1)

            over_units(pe, unit)


def inner(v, r=0, c=0):
    return v.rearrange("p (i h w) -> p i h w", i=2, h=H + 2)[:, :, 1 + r:1 + r + H, 1 + c:1 + c + W]


def rows(v):
    return v.rearrange("p (i h w) -> p i h w", i=2, h=H)


def softplus_dve(nc, dve, sp, rs, step, exp_done, ln_done):
    col = lambda i: sp[:, i:i + 1]
    n = [0]

    def then(ins):
        n[0] += 1
        ins.then_inc(step, 1)
        dve.wait_ge(step, n[0])

    then(nc.vector.tensor_scalar(col(1), rs, -1.0, None, ALU.mult))
    then(nc.vector.tensor_tensor(col(1), col(1), rs, ALU.min))
    dve.wait_ge(exp_done, 1)
    then(nc.vector.tensor_scalar(col(3), col(2), 1.0, None, ALU.add))
    dve.wait_ge(ln_done, 1)
    then(nc.vector.tensor_scalar(col(5), col(3), -1.0, None, ALU.add))
    then(nc.vector.tensor_scalar(col(6), col(5), 0.0, None, ALU.is_equal))
    then(nc.vector.tensor_tensor(col(5), col(5), col(6), ALU.add))
    then(nc.vector.tensor_tensor(col(4), col(4), col(6), ALU.add))
    then(nc.vector.reciprocal(col(5), col(5)))
    then(nc.vector.tensor_tensor(col(4), col(4), col(5), ALU.mult))
    then(nc.vector.tensor_tensor(col(4), col(4), col(2), ALU.mult))
    then(nc.vector.tensor_scalar(col(0), rs, 0.0, None, ALU.max))
    then(nc.vector.tensor_tensor(col(0), col(0), col(4), ALU.add))


def softplus_act(nc, act, sp, step, exp_done, ln_done):
    act.wait_ge(step, 2)
    nc.scalar.activation(sp[:, 2:3], sp[:, 1:2], ACT.Exp).then_inc(exp_done, 1)
    act.wait_ge(step, 3)
    nc.scalar.activation(sp[:, 4:5], sp[:, 3:4], ACT.Ln).then_inc(ln_done, 1)


def conv3(nc, w3, y, stats, mv, tmp, coef, pv, y3_t):
    with ExitStack() as c:
        sb = lambda name, shape, dt: c.enter_context(nc.sbuf_tensor(name, shape, dt))
        sem = lambda name: c.enter_context(nc.semaphore(name))
        w_f = sb("c_w", [P, MT, C_IN], F32)
        w_hi = sb("c_w_hi", [P, MT, C_IN], F32R)
        w_lo = sb("c_w_lo", [P, MT, C_IN], F32R)
        z_f = sb("c_z", [P, 2, MT, COLS], F32)
        z_hi = sb("c_z_hi", [P, 2, MT, COLS], F32R)
        z_lo = sb("c_z_lo", [P, 2, MT, COLS], F32R)
        y3s = sb("c_y3", [P, 2, KT, COLS], F32)
        stats3 = sb("c_stats3", [P, KT, PAIRS, 6], F32)
        ps = c.enter_context(nc.psum_tensor("c_ps", [P, 8, 512], F32))
        w_in, w_split = sem("c_w_in"), sem("c_w_split")
        bn_step, sqrt_in, sqrt_out, bn_done = sem("c_bn_step"), sem("c_sqrt_in"), sem("c_sqrt_out"), sem("c_bn_done")
        z_done, lo_done = sem("c_z_done"), sem("c_lo_done")
        conv_done, y_done = sem("c_conv_done"), sem("c_y_done")
        stored = [sem(f"c_stored{s}") for s in range(2)]
        agg = sem("c_agg")
        block = c.enter_context(nc.Block())

        @block.sync
        def _(sync):
            sync.dma_start(w_f[:, :, :], w3.rearrange("(t p) m -> p t m", p=P)).then_inc(w_in, 16)

            def body(i, last):
                for s in range(2):
                    sync.wait_ge(y_done, (i * 2 + s + 1) * KT)
                    sync.dma_start(y3_t[:, :, bass.ds((i * 2 + s) * COLS, COLS)], y3s[:, s, :, :])\
                        .then_inc(stored[s], 16)

            over_bodies(sync, body)
            for s in range(2):
                sync.wait_ge(stored[s], BODIES * 16)

        @block.scalar
        def _(act):
            act.wait_ge(sqrt_in, 1)
            nc.scalar.activation(tmp[:, 1, 0:MT], tmp[:, 0, 0:MT], ACT.Sqrt).then_inc(sqrt_out, 1)
            act.wait_ge(bn_done, 1)

            def z(n, s):
                for m in range(MT):
                    src = y[:, m, bass.ds(n * COLS, COLS)]
                    sc, sh = coef[:, m, 0:1], coef[:, m, 1:2]
                    nc.scalar.activation(z_f[:, s, m, :], src, ACT.Relu, bias=sh, scale=sc)
                    nc.scalar.activation(z_hi[:, s, m, :], src, ACT.Relu, bias=sh, scale=sc).then_inc(z_done, 1)

            for s in range(2):
                z(s, s)

            def body(i, first, last):
                for s in range(2):
                    if not first:
                        act.wait_ge(stored[s], i * 16)
                    for m in range(KT):
                        act.wait_ge(conv_done, (i * 2 + s) * KT + m + 1)
                        nc.scalar.activation(y3s[:, s, m, :], ps[:, 4 * s + m % 4, 0:COLS],
                                             ACT.Copy).then_inc(y_done, 1)
                    if not last:
                        z(i * 2 + s + 2, s)

            body(0, True, False)
            with act.Fori(1, BODIES - 1) as i:
                body(i, False, False)
            body(BODIES - 1, False, True)

        @block.vector
        def _(dve):
            step = 0
            for m in range(MT):
                nc.vector.bn_aggr(mv[:, m, :], stats[:, m, :, :].rearrange("p a b -> p (a b)")).then_inc(bn_step, 1)
                step += 1
            dve.wait_ge(bn_step, step)
            step = bn_coefficients(nc, dve, bn_step, step, coef[:, 0:MT, 0], coef[:, 0:MT, 1], mv, tmp,
                                   pv("b2"), pv("g2"), pv("be2"), MT, sqrt_in, sqrt_out)
            nc.vector.memset(tmp[:, 2, 0:1], 0.0).then_inc(bn_done, 1)
            dve.wait_ge(w_in, 16)
            split(nc, dve, w_hi[:, :, :], w_lo[:, :, :], w_f[:, :, :], w_split, 0)

            def lo(n, s):
                dve.wait_ge(z_done, n * 2 + MT)
                nc.vector.tensor_tensor(z_lo[:, s, :, :], z_f[:, s, :, :], z_hi[:, s, :, :].bitcast(F32),
                                        ALU.subtract).then_inc(lo_done, 1)

            for s in range(2):
                lo(s, s)

            def body(i, last):
                for s in range(2):
                    for m in range(KT):
                        dve.wait_ge(y_done, (i * 2 + s) * KT + m + 1)
                        nc.vector.bn_stats(stats3[:, m, bass.ds(i * 2 + s, 1), :].rearrange("p a b -> p (a b)"),
                                           y3s[:, s, m, :])
                    if not last:
                        lo(i * 2 + s + 2, s)

            over_bodies(dve, body)
            nc.vector.memset(tmp[:, 3, 0:1], 0.0).then_inc(bn_step, 1)
            dve.wait_ge(bn_step, step + 1)
            for m in range(KT):
                nc.vector.bn_aggr(mv[:, m, :], stats3[:, m, :, :].rearrange("p a b -> p (a b)")).then_inc(agg, 1)

        @block.tensor
        def _(pe):
            pe.wait_ge(w_split, 2)

            def body(i, last):
                for s in range(2):
                    pe.wait_ge(lo_done, i * 2 + s + 1)
                    for m in range(KT):
                        if m >= 4:
                            pe.wait_ge(y_done, (i * 2 + s) * KT + m - 3)
                        steps = [(w, v, k) for k in range(MT) for w, v in ((w_hi, z_hi), (w_lo, z_hi), (w_hi, z_lo))]
                        for at, (w, v, k) in enumerate(steps):
                            last_mm = nc.tensor.matmul(ps[:, 4 * s + m % 4, 0:COLS], w[:, k, m * P:(m + 1) * P],
                                                       v[:, s, k, :], start=at == 0, stop=at == len(steps) - 1)
                        last_mm.then_inc(conv_done, 1)

            over_bodies(pe, body)


def diagonal(a, c, n, start):
    length, stride = a.shape[1], P - GC
    if c == KT - 1:
        parts = ((0, KT // 2, GC * c), (KT // 2, KT // 2, GC * c + KT // 2 * stride))
    else:
        parts = ((0, KT - 1 - c, P * (c + 1) + stride), (KT - 1 - c, c + 1, GC * c))
    for q, count, row in parts:
        first = a[row:row + 1, bass.ds(start, n)]
        yield q * GC, count * GC, bass.AP(a.tensor, first.offset, [[stride * length, count], [length, GC], [1, n]])


def later(at, d):
    p, i, s = at
    i, s = (i + 1, s) if d == 2 else (i + s, 1 - s)
    if isinstance(i, int) and i == BODIES:
        p, i = p + 1, 0
    return (p, i, s) if p < PASSES else None


def before(at):
    p, i, s = at
    if s:
        return p, i, 0
    if isinstance(i, int) and i == 0:
        return (p - 1, BODIES - 1, 1) if p else None
    return p, i - 1, 1


def over_steps(engine, step):
    for p in range(PASSES):
        for s in range(2):
            step((p, 0, s))
        with engine.Fori(1, BODIES - 1) as i:
            for s in range(2):
                step((p, i, s))
        for s in range(2):
            step((p, BODIES - 1, s))


def layer1(nc, x, x_t, y3, y3_t, out_t, wmain, wside, wout_a, wout_b, mv, tmp, coef, pv, sp):
    coef_dram = nc.dram_tensor("coef_spill", [C_IN, 2], F32).ap()
    with ExitStack() as c:
        sb = lambda name, shape, dt: c.enter_context(nc.sbuf_tensor(name, shape, dt))
        sem = lambda name: c.enter_context(nc.semaphore(name))
        bank = lambda name: c.enter_context(nc.psum_tensor(name, [P, 512], F32))
        coef_sk = sb("d_coef_sk", [P, KT, 2], F32)
        w_raw = sb("d_w_raw", [P, WPP * P], F32)
        w_main_hi, w_main_lo, w_side, w_side_lo, w_out = (
            [sb(f"d_w_{name}{s}", [P, n, P], F32R) for s in range(2)]
            for name, n in (("main_hi", WPP), ("main_lo", WPP), ("side", WPP), ("side_lo", WPP // 2), ("out", WPP)))
        x_win = sb("d_x_win", [P, 2, WT, COLS], F32)
        y_win = sb("d_y_win", [P, 2, WT, COLS], F32)
        x_res = sb("d_x_res", [P, 2, 2, COLS], F32)
        y_res = sb("d_y_res", [P, 2, 2, COLS], F32)
        v_hi = sb("d_v_hi", [P, 2, WT, PAD], F32R)
        v_lo = sb("d_v_lo", [P, 2, WT, PAD], F32R)
        low = sb("d_low", [P, 2, 2, PAD], F32R)
        upp = sb("d_upp", [P, 2, 2, PAD], F32R)
        low3 = sb("d_low3", [P, 2, 2, PAD], F32R)
        upp3 = sb("d_upp3", [P, 2, 2, PAD], F32R)
        h_f = sb("d_h", [P, BANKS, COLS], F32)
        h_hi = sb("d_h_hi", [P, HB, COLS], F32R)
        h_lo = sb("d_h_lo", [P, HB, COLS], F32R)
        part = sb("d_part", [P, 2, COLS], F32)
        res = sb("d_res", [P, 4, COLS], F32)
        hid = [bank(f"d_hid{b}") for b in range(BANKS)]
        acc = [[bank(f"d_acc{oo}{h}") for h in range(2)] for oo in range(2)]

        raw_in, w_step, pads_done = sem("d_raw_in"), sem("d_w_step"), sem("d_pads_done")
        sk_in, bn_step, sqrt_in, sqrt_out, bn_done = (
            sem(f"d_{n}") for n in ("sk_in", "bn_step", "sqrt_in", "sqrt_out", "bn_done"))
        win_in, res_in, low_in, upp_in, low3_in, upp3_in = (
            [sem(f"d_{n}_in{s}") for s in range(2)] for n in ("win", "res", "low", "upp", "low3", "upp3"))
        win_sum, win_relu, win_lo = sem("d_win_sum"), sem("d_win_relu"), sem("d_win_lo")
        res_sum, res_relu = sem("d_res_sum"), sem("d_res_relu")
        first_done, h_done, hi_done, lo_done = (
            sem(f"d_{n}") for n in ("first_done", "h_done", "hi_done", "lo_done"))
        oct_done, part_done, comb_done, fin_done = (
            sem(f"d_{n}") for n in ("oct_done", "part_done", "comb_done", "fin_done"))
        stored = [sem(f"d_stored{o}") for o in range(4)]
        block = c.enter_context(nc.Block())

        number = lambda at: at[1] * 2 + (at[0] * PAIRS + at[2])
        pair = lambda at: at[1] * 2 + at[2]
        fills = lambda at: at[1] + (at[0] * BODIES + 1)

        @block.sync
        def _(sync):
            def load_window(at):
                p, _, s = at
                third = (2 * p + 2) % KT
                cols = bass.ds(pair(at) * COLS, COLS)
                for dst, src in ((x_win, x_t), (y_win, y3_t)):
                    sync.dma_start(dst[:, s, 0:2, :], src[:, 2 * p:2 * p + 2, cols]).then_inc(win_in[s], 16)
                    sync.dma_start(dst[:, s, 2, :], src[:, third, cols]).then_inc(win_in[s], 16)

            def load_residual(at):
                p, _, s = at
                for oo in range(2):
                    for dst, src in ((x_res, x), (y_res, y3)):
                        for first, count, pattern in diagonal(src, 2 * p + oo, COLS, pair(at) * COLS):
                            sync.dma_start(dst[first:first + count, s, oo, :], pattern).then_inc(res_in[s], 16)

            def load_stacks(at):
                s = at[2]
                sync.wait_ge(win_lo, (number(at) + 1) * WT)
                for dst, done, row, t, parts in ((low3, low3_in, 0, 1, (v_hi, v_hi, v_lo)),
                                                 (low, low_in, 0, 1, (v_hi, v_lo)),
                                                 (upp, upp_in, P // 2, 0, (v_hi, v_lo)),
                                                 (upp3, upp3_in, P - QUARTER, 0, (v_hi, v_hi, v_lo))):
                    size = QUARTER if len(parts) == 3 else P // 2
                    for n, src in enumerate(parts):
                        sync.dma_start(dst[n * size:(n + 1) * size, s, :, :].bitcast(F32),
                                       src[row:row + size, s, t:t + 2, :].bitcast(F32)).then_inc(done[s], 16)

            def load_raw(p, stage):
                if p or stage:
                    sync.wait_ge(w_step, W_STEPS * p + W_STAGES[stage])
                if stage < 2:
                    src = (wmain, wside)[stage]
                    sync.dma_start(w_raw[:, :], src[:, p * WPP * P:(p + 1) * WPP * P]).then_inc(raw_in, 16)
                else:
                    first = (p * WPP + (stage - 2) * OCT) * P
                    for n, src in enumerate((wout_a, wout_b)):
                        sync.dma_start(w_raw[:, n * OCT * P:(n + 1) * OCT * P], src[:, first:first + OCT * P])\
                            .then_inc(raw_in, 16)

            def store(at, oo):
                o = 2 * at[2] + oo
                sync.wait_ge(fin_done, number(at) * 2 + oo + 1)
                sync.dma_start(out_t[:, 2 * at[0] + oo, bass.ds(pair(at) * COLS, COLS)], res[:, o, :])\
                    .then_inc(stored[o], 16)

            load_window((0, 0, 0))
            load_raw(0, 0)
            load_raw(0, 1)
            load_stacks((0, 0, 0))
            load_raw(0, 2)
            load_window((0, 0, 1))
            load_raw(0, 3)
            load_residual((0, 0, 0))
            sync.wait_ge(bn_done, 1)
            sync.dma_start(coef_dram.rearrange("(t p) a -> p t a", p=P), coef[:, :, :]).then_inc(stored[3], 16)
            sync.wait_ge(stored[3], 16)
            for tile in range(KT):
                for first, count, pattern in diagonal(coef_dram, tile, 2, 0):
                    sync.dma_start(coef_sk[first:first + count, tile, :], pattern).then_inc(sk_in, 16)

            def step(at):
                p, i, s = at
                prepare = isinstance(i, int) and p + 1 < PASSES
                if prepare and i == 0:
                    load_raw(p + 1, s)
                if (then := later(at, 2)) is not None:
                    sync.wait_ge(win_lo, (number(at) + 1) * WT)
                    load_window(then)
                then = later(at, 1)
                if then is not None:
                    load_stacks(then)
                if (prev := before(at)) is not None:
                    store(prev, 1)
                if then is not None:
                    load_residual(then)
                store(at, 0)
                if prepare and (i, s) in ((0, 1), (BODIES - 1, 0)):
                    load_raw(p + 1, 3 - s)

            over_steps(sync, step)
            store((PASSES - 1, BODIES - 1, 1), 1)
            for o in range(4):
                sync.wait_ge(stored[o], 16 * (PASSES * BODIES + (o == 3)))

        @block.gpsimd
        def _(pool):
            nc.gpsimd.memset(v_hi[:, :, :, :].bitcast(F32), 0.0).then_inc(pads_done, 1)
            nc.gpsimd.memset(v_lo[:, :, :, :].bitcast(F32), 0.0).then_inc(pads_done, 1)

            def window_lo(at, t):
                s = at[2]
                pool.wait_ge(win_relu, number(at) * WT + t + 1)
                nc.gpsimd.tensor_tensor(inner(v_lo[:, s, t, :]), rows(x_win[:, s, t, :]),
                                        inner(v_hi[:, s, t, :]).bitcast(F32), ALU.subtract).then_inc(win_lo, 1)

            def finish(at, oo):
                o = 2 * at[2] + oo
                pool.wait_ge(comb_done, number(at) * 2 + oo + 1)
                pool.wait_ge(res_relu, number(at) * 2 + oo + 1)
                nc.gpsimd.tensor_tensor(res[:, o, :], res[:, o, :], x_res[:, at[2], oo, :],
                                        ALU.add).then_inc(fin_done, 1)

            for t in range(WT):
                window_lo((0, 0, 0), t)

            def step(at):
                if (then := later(at, 1)) is not None:
                    for t in range(WT):
                        window_lo(then, t)
                if (prev := before(at)) is not None:
                    finish(prev, 1)
                finish(at, 0)

            over_steps(pool, step)
            finish((PASSES - 1, BODIES - 1, 1), 1)

        @block.scalar
        def _(act):
            act.wait_ge(sqrt_in, 1)
            nc.scalar.activation(tmp[:, 1, :], tmp[:, 0, :], ACT.Sqrt).then_inc(sqrt_out, 1)
            act.wait_ge(bn_done, 1)
            act.wait_ge(pads_done, 2)

            def window_tile(at, t):
                p, _, s = at
                shift = coef[:, (2 * p + t) % KT, 1:2]
                act.wait_ge(win_sum, number(at) * WT + t + 1)
                nc.scalar.activation(inner(v_hi[:, s, t, :]), rows(y_win[:, s, t, :]), ACT.Relu, bias=shift)
                nc.scalar.activation(x_win[:, s, t, :], y_win[:, s, t, :], ACT.Relu, bias=shift).then_inc(win_relu, 1)

            def residual_tile(at, oo):
                p, _, s = at
                act.wait_ge(res_sum, number(at) * 2 + oo + 1)
                nc.scalar.activation(x_res[:, s, oo, :], y_res[:, s, oo, :], ACT.Relu,
                                     bias=coef_sk[:, 2 * p + oo, 1:2]).then_inc(res_relu, 1)

            def move_low_parts(at, oo):
                act.wait_ge(oct_done, number(at) * 2 + oo + 1)
                nc.scalar.activation(part[P // 2:P, oo, :], acc[oo][0][0:P // 2, 0:COLS], ACT.Copy)
                nc.scalar.activation(part[0:P // 2, oo, :], acc[oo][1][P // 2:P, 0:COLS], ACT.Copy)\
                    .then_inc(part_done, 1)

            for t in range(WT):
                window_tile((0, 0, 0), t)

            def step(at):
                p = at[0]
                hb = pv("hid_b")
                for g in range(WPP):
                    k, b = p * WPP + g, g % BANKS
                    act.wait_ge(first_done, number(at) * WPP + g + 1)
                    if g >= BANKS or before(at) is not None:
                        act.wait_ge(lo_done, number(at) * (WPP // 2) + g // 2 - BANKS // 2 + 1)
                    nc.scalar.activation(h_f[:, b, :], hid[b][:, 0:COLS], ACT.Relu,
                                         bias=hb[:, k:k + 1]).then_inc(h_done, 1)
                    if g in (0, 1, 2) and (then := later(at, 1)) is not None:
                        window_tile(then, g)
                    if g in (9, 11):
                        residual_tile(at, g // 2 - 4)
                    if g == 5 and (prev := before(at)) is not None:
                        move_low_parts(prev, 1)
                    if g == 13:
                        move_low_parts(at, 0)

            over_steps(act, step)
            move_low_parts((PASSES - 1, BODIES - 1, 1), 1)

        @block.vector
        def _(dve):
            for tile in (low3, upp3):
                nc.vector.memset(tile[3 * QUARTER:P, :, :, :].bitcast(F32), 0.0)
            bn_coefficients(nc, dve, bn_step, 0, coef[:, :, 0], coef[:, :, 1], mv, tmp, pv("b3"), pv("g3"),
                            pv("be3"), KT, sqrt_in, sqrt_out, by=sp[:, 0:1])
            nc.vector.memset(sp[:, 7:8], 0.0).then_inc(bn_done, 1)
            dve.wait_ge(pads_done, 2)

            def window_sum(at, t):
                p, _, s = at
                dve.wait_ge(win_in[s], fills(at) * 64)
                nc.vector.scalar_tensor_tensor(y_win[:, s, t, :], y_win[:, s, t, :], coef[:, (2 * p + t) % KT, 0:1],
                                               x_win[:, s, t, :], op0=ALU.mult, op1=ALU.add).then_inc(win_sum, 1)

            def residual_sum(at, oo):
                p, _, s = at
                dve.wait_ge(res_in[s], fills(at) * 128)
                nc.vector.scalar_tensor_tensor(y_res[:, s, oo, :], y_res[:, s, oo, :],
                                               coef_sk[:, 2 * p + oo, 0:1], x_res[:, s, oo, :],
                                               op0=ALU.mult, op1=ALU.add).then_inc(res_sum, 1)

            def combine(at, oo):
                p, _, s = at
                o = 2 * s + oo
                dve.wait_ge(part_done, number(at) * 2 + oo + 1)
                if o == 3:
                    dve.wait_ge(stored[o], fills(at) * 16)
                elif not (isinstance(at[1], int) and p == at[1] == 0):
                    dve.wait_ge(stored[o], fills(at) * 16 - 16)
                for half, h in ((slice(P // 2, P), 0), (slice(0, P // 2), 1)):
                    ins = nc.vector.scalar_tensor_tensor(
                        res[half, o, :], acc[oo][h][half, 0:COLS], pv("out_b")[half, 2 * p + oo:2 * p + oo + 1],
                        part[half, oo, :], op0=ALU.add, op1=ALU.add)
                ins.then_inc(comb_done, 1)

            def weights(p, stage):
                b, count = p % 2, W_STEPS * p + W_STAGES[stage]
                raw = w_raw[:, :].rearrange("p (g m) -> p g m", m=P)
                octets = lambda a: a.rearrange("p (o j) m -> p o j m", o=2)
                dve.wait_ge(raw_in, 96 * p + (16, 32, 64, 96)[stage])

                def then(ins):
                    nonlocal count
                    count += 1
                    ins.then_inc(w_step, 1)
                    dve.wait_ge(w_step, count)

                if stage == 0:
                    then(nc.vector.tensor_copy(w_main_hi[b][:, :, :], raw))
                    then(nc.vector.tensor_tensor(w_main_lo[b][:, :, :], raw, w_main_hi[b][:, :, :].bitcast(F32),
                                                 ALU.subtract))
                elif stage == 1:
                    then(nc.vector.tensor_copy(w_side[b][:, :, :], raw))
                    hi, half = octets(w_side[b][:, :, :]), slice(2, 6)
                    then(nc.vector.tensor_tensor(octets(w_side_lo[b][:, :, :]), octets(raw)[:, :, half, :],
                                                 hi[:, :, half, :].bitcast(F32), ALU.subtract))
                    second = slice(QUARTER, 2 * QUARTER)
                    for js in (slice(0, 2), slice(6, 8)):
                        then(nc.vector.tensor_tensor(hi[second, :, js, :], octets(raw)[second, :, js, :],
                                                     hi[second, :, js, :].bitcast(F32), ALU.subtract))
                else:
                    w = w_out[b][:, (stage - 2) * OCT:(stage - 1) * OCT, :]
                    raw_a, raw_b = raw[:, 0:OCT, :], raw[:, OCT:2 * OCT, :]
                    then(nc.vector.tensor_copy(w, raw_b))
                    then(nc.vector.tensor_tensor(raw_b, raw_b, w.bitcast(F32), ALU.subtract))
                    then(nc.vector.tensor_copy(w, raw_a))
                    then(nc.vector.tensor_tensor(w, w.bitcast(F32), raw_b, ALU.add))

            for t in range(WT):
                window_sum((0, 0, 0), t)
            for stage in range(4):
                weights(0, stage)
            for t in range(WT):
                window_sum((0, 0, 1), t)
            dve.wait_ge(sk_in, 2 * KT * 16)

            def step(at):
                p, i, s = at
                for g in range(0, WPP, 2):
                    b, f = g % HB, g % BANKS
                    count = number(at) * (WPP // 2) + g // 2 + 1
                    dve.wait_ge(h_done, number(at) * WPP + g + 2)
                    nc.vector.tensor_copy(h_hi[:, b:b + 2, :], h_f[:, f:f + 2, :]).then_inc(hi_done, 1)
                    if g == 6 and (prev := before(at)) is not None:
                        combine(prev, 1)
                    if g == 8:
                        residual_sum(at, 0)
                        residual_sum(at, 1)
                    if g in (10, 12, 14) and (then := later(at, 2)) is not None:
                        window_sum(then, g // 2 - 5)
                    if g == 14:
                        combine(at, 0)
                    if isinstance(i, int) and p + 1 < PASSES and g == 12:
                        weights(p + 1, s if i == 0 else 2 + s)
                    dve.wait_ge(hi_done, count)
                    nc.vector.tensor_tensor(h_lo[:, b:b + 2, :], h_f[:, f:f + 2, :],
                                            h_hi[:, b:b + 2, :].bitcast(F32), ALU.subtract).then_inc(lo_done, 1)

            over_steps(dve, step)
            combine((PASSES - 1, BODIES - 1, 1), 1)

        @block.tensor
        def _(pe):
            def first_product(at, g):
                p, i, s = at
                b, k = p % 2, p * WPP + g
                oo, j = divmod(g, OCT)
                quarter = j in (0, 1, 6, 7)
                if g == 0:
                    if isinstance(i, int) and (i, s) == (0, 0):
                        pe.wait_ge(w_step, W_STEPS * p + W_STAGES[2])
                    pe.wait_ge(win_lo, (number(at) + 1) * WT)
                if g in (0, 2, 4, 6):
                    pe.wait_ge((low3_in, low_in, upp_in, upp3_in)[g // 2][s], fills(at) * (48 if quarter else 32))
                if g >= BANKS or before(at) is not None:
                    pe.wait_ge(h_done, number(at) * WPP + g - BANKS + 1)
                if j < OCT // 2:
                    main, side, main_tile, side_tile = oo, low3 if quarter else low, 0, 1
                else:
                    main, side, main_tile, side_tile = oo + 1, upp3 if quarter else upp, 1, 0
                at_main, at_side = (SHIFTS[shift_of(k, t)] for t in (main_tile, side_tile))
                products = [(w_main_hi, g, v_hi[:, s, main, :], at_main), (w_main_lo, g, v_hi[:, s, main, :], at_main),
                            (w_main_hi, g, v_lo[:, s, main, :], at_main), (w_side, g, side[:, s, oo, :], at_side)]
                if not quarter:
                    products.append((w_side_lo, 4 * oo + j - 2, side[:, s, oo, :], at_side))
                for n, (w, at_w, v, shift) in enumerate(products):
                    ins = nc.tensor.matmul(hid[g % BANKS][:, 0:COLS], w[b][:, at_w, :], inner(v, *shift),
                                           start=n == 0, stop=n == len(products) - 1)
                ins.then_inc(first_done, 1)

            def second_product(at, g):
                p = at[0]
                oo, j = divmod(g, OCT)
                if j == 0 and isinstance(at[1], int) and at[1] == at[2] == 0:
                    pe.wait_ge(w_step, W_STEPS * p + W_STAGES[3 + oo])
                pe.wait_ge(lo_done, number(at) * (WPP // 2) + g // 2 + 1)
                h, q = divmod(j, OCT // 2)
                for n, v in enumerate((h_hi, h_lo)):
                    ins = nc.tensor.matmul(acc[oo][h][:, 0:COLS], w_out[p % 2][:, g, :], v[:, g % HB, :],
                                           start=q == n == 0, stop=q == OCT // 2 - 1 and n == 1)
                if j == OCT - 1:
                    ins.then_inc(oct_done, 1)

            for g in range(LAG):
                first_product((0, 0, 0), g)

            def step(at):
                for g in range(0, WPP, 2):
                    for g1 in (g + LAG, g + LAG + 1):
                        if g1 < WPP:
                            first_product(at, g1)
                        elif (then := later(at, 1)) is not None:
                            first_product(then, g1 - WPP)
                    second_product(at, g)
                    second_product(at, g + 1)

            over_steps(pe, step)


def window_weights(w1, w2, b2):
    main, side, out_a, out_b = (np.zeros((GROUPS, P, P), w1.dtype) for _ in range(4))
    bias = np.zeros((P, KT), b2.dtype)
    for k in range(GROUPS):
        m, (c, j) = group_of(k), divmod(k, OCT)
        w, cut = w1[m].T, P - GC * j
        if j < OCT // 2:
            main[k, GC * j:] = w[:cut]
            rest, first = w[cut:], 0
        else:
            main[k, :GC * (j + 1)] = w[cut:]
            rest, first = w[:cut], -cut
        size = QUARTER if len(rest) <= QUARTER else P // 2
        for start in range(0, 3 * QUARTER, size):
            at = start + first % size
            side[k, at:at + len(rest)] = rest
        q = GC * (OCT - 1 - j)
        out_a[k, :, q:q + GC] = w2[m].T
        out_b[k, :, (q + P // 2) % P:(q + P // 2) % P + GC] = w2[m].T
        bias[q:q + GC, c] = b2[GC * m:GC * (m + 1)]
    by_row = lambda a: np.ascontiguousarray(a.transpose(1, 0, 2)).reshape(P, GROUPS * P)
    return by_row(main), by_row(side), by_row(out_a), by_row(out_b), bias


def kernel(x, L0_conv_w1, L0_conv_b1, L0_conv_g1, L0_conv_be1, L0_conv_w2, L0_conv_b2, L0_conv_g2, L0_conv_be2,
           L0_conv_w3, L0_conv_b3, L0_conv_g3, L0_conv_be3, L0_conv_residual_scale, L1_conv_w1, L1_conv_b1,
           L1_conv_w2, L1_conv_b2):
    import concourse.bacc as bacc
    from concourse.bass_utils import run_bass_kernel_spmd

    wmain, wside, wout_a, wout_b, out_b = window_weights(np.asarray(L1_conv_w1), np.asarray(L1_conv_w2),
                                                         np.asarray(L1_conv_b2))
    by_tile = lambda a: np.asarray(a).reshape(-1, P).T
    hid_b = np.asarray(L1_conv_b1).reshape(GROUPS, HID)[[group_of(k) for k in range(GROUPS)]].T
    vectors = [by_tile(a) for a in (L0_conv_b1, L0_conv_g1, L0_conv_be1, L0_conv_b2, L0_conv_g2, L0_conv_be2,
                                    L0_conv_b3, L0_conv_g3, L0_conv_be3)]
    vectors += [np.repeat(np.asarray(L0_conv_residual_scale).reshape(1, 1), P, 0), hid_b, out_b]
    arrays = {
        "x": np.asarray(x).transpose(1, 0, 2, 3).reshape(C_IN, T),
        "w1": np.asarray(L0_conv_w1).reshape(C_MID, C_IN).T,
        "w2": np.asarray(L0_conv_w2).reshape(C_MID, C_MID, 9).transpose(1, 2, 0),
        "w3": np.asarray(L0_conv_w3).reshape(C_IN, C_MID).T,
        "wmain": wmain, "wside": wside, "wout_a": wout_a, "wout_b": wout_b,
        "params": np.concatenate(vectors, axis=1),
    }
    arrays = {f"{name}_dram": np.ascontiguousarray(a) for name, a in arrays.items()}
    nc = bacc.Bacc("TRN2", target_bir_lowering=False, num_devices=1)
    args = [nc.dram_tensor(name, a.shape, mybir.dt.from_np(a.dtype), kind="ExternalInput").ap()
            for name, a in arrays.items()]
    out = nc.dram_tensor("out_dram", [C_IN, T], F32, kind="ExternalOutput").ap()
    build(nc, *args, out)
    got = run_bass_kernel_spmd(nc, [arrays], core_ids=[0]).results[0]["out_dram"]
    got = np.asarray(got).reshape(KT, OCT, GC, N_IMG, H, W)
    result = np.empty((KT, OCT, GC, N_IMG, H, W), got.dtype)
    for c in range(KT):
        for q in range(OCT):
            result[(c - OCT + 1 + q) % KT, OCT - 1 - q] = got[c, q]
    return np.ascontiguousarray(result.reshape(C_IN, N_IMG, H, W).transpose(1, 0, 2, 3))
```

```python
from contextlib import ExitStack

import numpy as np

import concourse.bass as bass
from concourse import mybir

F32 = mybir.dt.float32
F32R = mybir.dt.float32r
ACT = mybir.ActivationFunctionType
ALU = mybir.AluOpType

P = 128
N_IMG, C_IN, H, W = 64, 1024, 14, 14
C_MID = 256
PAIRS = N_IMG // 2
COLS = 2 * H * W
T = N_IMG * H * W
PAD = 2 * (H + 2) * (W + 2)
KT = C_IN // P
MT = C_MID // P
BODIES = PAIRS // 2
TAPS = [(r, c) for r in (-1, 0, 1) for c in (-1, 0, 1)]
BN_EPS = 1e-5

GROUPS, GC, HID = 64, 16, 128
SHIFTS = [(0, 0)] + [t for t in TAPS if t != (0, 0)]
PASSES = 4
WPP = GROUPS // PASSES
WT = 3
OCT = 8
LAG = 6
BANKS = 4
HB = 8
QUARTER = P // 4
STAGES = 4
STEPS = 4
W_AT = (8, 10, 12, 14)


def group_of(k):
    return pow(9, -1, GROUPS) * k % GROUPS


def shift_of(k, tile):
    s = (9 * group_of(k) * GC) // C_IN
    return s + 1 if tile and k // OCT + 1 == KT else s


PARAMS = {}
_at = 0
for _name, _n in (("b1", MT), ("g1", MT), ("be1", MT), ("b2", MT), ("g2", MT), ("be2", MT),
                  ("b3", KT), ("g3", KT), ("be3", KT), ("rs", 1), ("hid_b", GROUPS), ("out_b", KT)):
    PARAMS[_name] = (_at, _at + _n)
    _at += _n
N_PARAMS = _at


def build(nc, x, w1, w2, w3, wmain, wside, wout_a, wout_b, params, out):
    y3 = nc.dram_tensor("y3_spill", [C_IN, T], F32).ap()
    x_t = x.rearrange("(t p) n -> p t n", p=P)
    y3_t = y3.rearrange("(t p) n -> p t n", p=P)
    out_t = out.rearrange("(t p) n -> p t n", p=P)

    with ExitStack() as ctx:
        par = ctx.enter_context(nc.sbuf_tensor("par", [P, N_PARAMS], F32))
        coef = ctx.enter_context(nc.sbuf_tensor("coef", [P, KT, 2], F32))
        mv = ctx.enter_context(nc.sbuf_tensor("mv", [P, KT, 2], F32))
        tmp = ctx.enter_context(nc.sbuf_tensor("tmp", [P, 4, KT], F32))
        sp = ctx.enter_context(nc.sbuf_tensor("sp", [P, 8], F32))
        par_in = ctx.enter_context(nc.semaphore("par_in"))

        def pv(name):
            a, b = PARAMS[name]
            return par[:, a:b]

        with ExitStack() as mid:
            y = mid.enter_context(nc.sbuf_tensor("y", [P, MT, T], F32))
            stats = mid.enter_context(nc.sbuf_tensor("stats", [P, MT, PAIRS, 6], F32))
            conv1(nc, x_t, w1, y, stats, par, params, par_in, pv, sp)
            conv2(nc, w2, y, stats, mv, tmp, coef, pv)
            conv3(nc, w3, y, stats, mv, tmp, coef, pv, y3_t)
        layer1(nc, x, x_t, y3, y3_t, out_t, (wmain, wside, wout_a, wout_b), mv, tmp, coef, pv, sp)


def split(nc, dve, hi, lo, v, done, count):
    nc.vector.tensor_copy(hi, v).then_inc(done, 1)
    dve.wait_ge(done, count + 1)
    nc.vector.tensor_tensor(lo, v, hi.bitcast(F32), ALU.subtract).then_inc(done, 1)
    return count + 2


def bn_coefficients(nc, dve, step, count, scale, shift, mv, tmp, b, g, be, n, sqrt_in, sqrt_out, by=None):
    def then(ins):
        nonlocal count
        count += 1
        ins.then_inc(step, 1)
        dve.wait_ge(step, count)

    mean, var = mv[:, 0:n, 0], mv[:, 0:n, 1]
    v, r, e, m = (tmp[:, i, 0:n] for i in range(4))
    then(nc.vector.tensor_tensor(m, mean, b, ALU.add))
    nc.vector.tensor_scalar(v, var, BN_EPS, None, ALU.add).then_inc(sqrt_in, 1)
    dve.wait_ge(sqrt_out, 1)
    then(nc.vector.reciprocal(r, r))
    then(nc.vector.tensor_tensor(e, v, r, ALU.mult))
    then(nc.vector.tensor_tensor(e, e, r, ALU.mult))
    then(nc.vector.tensor_scalar(e, e, -0.5, 1.5, ALU.mult, ALU.add))
    then(nc.vector.tensor_tensor(r, r, e, ALU.mult))
    then(nc.vector.tensor_tensor(scale, r, g, ALU.mult))
    then(nc.vector.tensor_tensor(m, b, m, ALU.subtract))
    then(nc.vector.tensor_tensor(m, m, scale, ALU.mult))
    then(nc.vector.tensor_tensor(shift, m, be, ALU.add))
    if by is not None:
        then(nc.vector.tensor_scalar(scale, scale, by, None, ALU.mult))
        then(nc.vector.tensor_scalar(shift, shift, by, None, ALU.mult))
    return count


def over_bodies(engine, body):
    with engine.Fori(0, BODIES - 1) as i:
        body(i, False)
    body(BODIES - 1, True)


def conv1(nc, x_t, w1, y, stats, par, params, par_in, pv, sp):
    with ExitStack() as c:
        sb = lambda name, shape, dt: c.enter_context(nc.sbuf_tensor(name, shape, dt))
        sem = lambda name: c.enter_context(nc.semaphore(name))
        w_f = sb("a_w", [P, KT, C_MID], F32)
        w_hi = sb("a_w_hi", [P, KT, C_MID], F32R)
        w_lo = sb("a_w_lo", [P, KT, C_MID], F32R)
        x_f = sb("a_x", [P, 2, KT, COLS], F32)
        x_hi = sb("a_x_hi", [P, 2, KT, COLS], F32R)
        x_lo = sb("a_x_lo", [P, 2, KT, COLS], F32R)
        ps = c.enter_context(nc.psum_tensor("a_ps", [P, 4, 512], F32))
        first_in = [sem(f"a_first_in{h}") for h in range(2)]
        w_split = sem("a_w_split")
        x_in = [sem(f"a_x_in{s}") for s in range(2)]
        hi_done, lo_done = sem("a_hi_done"), sem("a_lo_done")
        conv_done, y_done = sem("a_conv_done"), sem("a_y_done")
        sp_step, sp_exp, sp_ln = sem("a_sp_step"), sem("a_sp_exp"), sem("a_sp_ln")
        block = c.enter_context(nc.Block())

        halves = (slice(0, KT // 2), slice(KT // 2, KT))

        @block.sync
        def _(sync):
            for h, half in enumerate(halves):
                sync.dma_start(w_f[:, half, :], w1.rearrange("(t p) m -> p t m", p=P)[:, half, :])\
                    .then_inc(first_in[h], 16)
                sync.dma_start(x_f[:, 0, half, :], x_t[:, half, 0:COLS]).then_inc(first_in[h], 16)

            def load(n, s):
                sync.dma_start(x_f[:, s, :, :], x_t[:, :, bass.ds(n * COLS, COLS)]).then_inc(x_in[s], 16)

            load(1, 1)
            sync.dma_start(par[:, :], params).then_inc(par_in, 16)

            def body(i, last):
                for s in range(2):
                    if not last:
                        sync.wait_ge(lo_done, i * 2 + s + 2)
                        load(i * 2 + s + 2, s)

            over_bodies(sync, body)
            sync.wait_ge(par_in, 16)

        @block.scalar
        def _(act):
            def hi(s, loads):
                act.wait_ge(x_in[s], loads * 16)
                nc.scalar.activation(x_hi[:, s, :, :], x_f[:, s, :, :], ACT.Copy).then_inc(hi_done, 1)

            for h, half in enumerate(halves):
                act.wait_ge(first_in[h], 2 * 16)
                nc.scalar.activation(x_hi[:, 0, half, :], x_f[:, 0, half, :], ACT.Copy).then_inc(hi_done, 1)
            hi(1, 1)
            softplus_act(nc, act, sp, sp_step, sp_exp, sp_ln)

            def body(i, last):
                for s in range(2):
                    for m in range(MT):
                        act.wait_ge(conv_done, i * 4 + 2 * s + m + 1)
                        nc.scalar.activation(y[:, m, bass.ds((i * 2 + s) * COLS, COLS)], ps[:, 2 * s + m, 0:COLS],
                                             ACT.Copy).then_inc(y_done, 1)
                    if not last:
                        hi(s, i + 1 + s)

            over_bodies(act, body)

        @block.vector
        def _(dve):
            for h, half in enumerate(halves):
                dve.wait_ge(first_in[h], 2 * 16)
                split(nc, dve, w_hi[:, half, :], w_lo[:, half, :], w_f[:, half, :], w_split, 2 * h)
                dve.wait_ge(hi_done, h + 1)
                nc.vector.tensor_tensor(x_lo[:, 0, half, :], x_f[:, 0, half, :], x_hi[:, 0, half, :].bitcast(F32),
                                        ALU.subtract).then_inc(lo_done, 1)

            def lo(s, n):
                dve.wait_ge(hi_done, n + 2)
                nc.vector.tensor_tensor(x_lo[:, s, :, :], x_f[:, s, :, :], x_hi[:, s, :, :].bitcast(F32),
                                        ALU.subtract).then_inc(lo_done, 1)

            lo(1, 1)
            dve.wait_ge(par_in, 16)
            softplus_dve(nc, dve, sp, pv("rs"), sp_step, sp_exp, sp_ln)

            def body(i, last):
                for s in range(2):
                    for m in range(MT):
                        dve.wait_ge(y_done, i * 4 + 2 * s + m + 1)
                        nc.vector.bn_stats(stats[:, m, bass.ds(i * 2 + s, 1), :].rearrange("p a b -> p (a b)"),
                                           y[:, m, bass.ds((i * 2 + s) * COLS, COLS)])
                    if not last:
                        lo(s, i * 2 + s + 2)

            over_bodies(dve, body)

        @block.tensor
        def _(pe):
            def products(s, ks, first, last):
                for m in range(MT):
                    steps = [(w, v, k) for k in ks for w, v in ((w_hi, x_hi), (w_lo, x_hi), (w_hi, x_lo))]
                    for at, (w, v, k) in enumerate(steps):
                        ins = nc.tensor.matmul(ps[:, 2 * s + m, 0:COLS], w[:, k, m * P:(m + 1) * P], v[:, s, k, :],
                                               start=first and at == 0, stop=last and at == len(steps) - 1)
                    if last:
                        ins.then_inc(conv_done, 1)

            def pair(n, s):
                pe.wait_ge(lo_done, n + 2)
                products(s, range(KT), True, True)

            for h in range(2):
                pe.wait_ge(w_split, 2 * h + 2)
                pe.wait_ge(lo_done, h + 1)
                products(0, range(KT)[halves[h]], h == 0, h == 1)
            pair(1, 1)
            with pe.Fori(1, BODIES) as i:
                for s in range(2):
                    pair(i * 2 + s, s)


def conv2(nc, w2, y, stats, mv, tmp, coef, pv):
    rows4 = 4 * (H // 2)
    v_cols = rows4 * (W + 2)
    units = N_IMG // 4
    with ExitStack() as c:
        sb = lambda name, shape, dt: c.enter_context(nc.sbuf_tensor(name, shape, dt))
        sem = lambda name: c.enter_context(nc.semaphore(name))
        w_hi = sb("b_w_hi", [P, MT, 4, 3, C_MID], F32R)
        w_lo = sb("b_w_lo", [P, MT, 4, 3, C_MID], F32R)
        w_f0 = sb("b_w_f0", [P, 3, 3, C_MID], F32)
        spare = sb("b_spare", [P, 6 * COLS], F32)
        w_f = (w_f0[:, :, :, :], spare[:, 0:9 * C_MID].rearrange("p (a b m) -> p a b m", a=3, b=3))
        m2_f, t1, t2 = (spare[:, n * MT * COLS:(n + 1) * MT * COLS].rearrange("p (m n) -> p m n", m=MT)
                        for n in range(3))
        z = sb("b_z", [P, MT * 4 * (H + 2) * (W + 2)], F32)
        v_f = sb("b_v", [P, MT, v_cols], F32)
        v_hi = sb("b_v_hi", [P, 4, MT, v_cols], F32R)
        v_lo = sb("b_v_lo", [P, 4, MT, v_cols], F32R)
        bank = [[c.enter_context(nc.psum_tensor(f"b_m{f}{m}", [P, 512], F32)) for m in range(MT)] for f in range(4)]
        w_in0 = [sem(f"b_w_in0{k}") for k in range(MT)]
        w_in = [sem(f"b_w_in{k}") for k in range(MT)]
        w_step, pads_done = sem("b_w_step"), sem("b_pads_done")
        bn_step, sqrt_in, sqrt_out, bn_done = sem("b_bn_step"), sem("b_sqrt_in"), sem("b_sqrt_out"), sem("b_bn_done")
        z_done, v_done, hi_done, lo_done = sem("b_z_done"), sem("b_v_done"), sem("b_hi_done"), sem("b_lo_done")
        mm_done, m2_done, t_done = sem("b_mm_done"), sem("b_m2_done"), sem("b_t_done")
        even_done, odd_done = sem("b_even_done"), sem("b_odd_done")
        block = c.enter_context(nc.Block())

        def over_units(engine, unit):
            unit(0, False)
            with engine.Fori(1, units - 1) as u:
                unit(u, False)
            unit(units - 1, True)

        @block.sync
        def _(sync):
            w2_t = w2.rearrange("(t p) (a b) m -> p t a b m", p=P, a=3)
            for k in range(MT):
                sync.dma_start(w_f[k][:, 0:1, :, :], w2_t[:, k, 0:1, :, :]).then_inc(w_in0[k], 16)
            for k in range(MT):
                sync.dma_start(w_f[k][:, 1:3, :, :], w2_t[:, k, 1:3, :, :]).then_inc(w_in[k], 16)

        @block.gpsimd
        def _(pool):
            nc.gpsimd.memset(z[:, :], 0.0).then_inc(pads_done, 1)
            z_rows = z[:, :].rearrange("p (i h w) -> p i h w", h=H + 2, w=W + 2)
            row = lambda a: z_rows[:, :, a:a + H - 1:2, :]
            v_rows = v_f[:, :, :].rearrange("p k (i h w) -> p (k i) h w", i=4, w=W + 2)

            def transform(u):
                pool.wait_ge(z_done, u + 1)
                for f, (a, b, op) in enumerate(((0, 2, ALU.subtract), (1, 2, ALU.add), (2, 1, ALU.subtract),
                                                (1, 3, ALU.subtract))):
                    if f or not (isinstance(u, int) and u == 0):
                        pool.wait_ge(lo_done, u * 4 + f)
                    nc.gpsimd.tensor_tensor(v_rows, row(a), row(b), op).then_inc(v_done, 1)

            transform(0)
            with pool.Fori(1, units) as u:
                transform(u)

        @block.scalar
        def _(act):
            act.wait_ge(sqrt_in, 1)
            nc.scalar.activation(tmp[:, 1, 0:MT], tmp[:, 0, 0:MT], ACT.Sqrt).then_inc(sqrt_out, 1)
            act.wait_ge(bn_done, 1)
            act.wait_ge(pads_done, 1)

            def relu(u):
                for k in range(MT):
                    src = y[:, k, bass.ds(u * 2 * COLS, 2 * COLS)].rearrange("p (i h w) -> p i h w", h=H, w=W)
                    dst = z[:, :].rearrange("p (k i h w) -> p k i h w", k=MT, h=H + 2, w=W + 2)
                    ins = nc.scalar.activation(dst[:, k, :, 1:1 + H, 1:1 + W], src, ACT.Relu, bias=coef[:, k, 1:2],
                                               scale=coef[:, k, 0:1])
                ins.then_inc(z_done, 1)

            def hi(u, f):
                act.wait_ge(v_done, u * 4 + f + 1)
                nc.scalar.activation(v_hi[:, f, :, :], v_f[:, :, :], ACT.Copy).then_inc(hi_done, 1)

            relu(0)
            for f in range(4):
                hi(0, f)

            def unit(u, last):
                if not last:
                    act.wait_ge(v_done, u * 4 + 4)
                    relu(u + 1)
                for f in range(4):
                    act.wait_ge(mm_done, u * 4 + f + 1)
                    if f == 2:
                        for m in range(MT):
                            nc.scalar.activation(m2_f[:, m, :], bank[2][m][:, 0:COLS], ACT.Copy).then_inc(m2_done, 1)
                    if not last:
                        hi(u + 1, f)

            over_units(act, unit)

        @block.vector
        def _(dve):
            step = 0
            for m in range(MT):
                nc.vector.bn_aggr(mv[:, m, :], stats[:, m, :, :].rearrange("p a b -> p (a b)")).then_inc(bn_step, 1)
                step += 1
            dve.wait_ge(bn_step, step)
            bn_coefficients(nc, dve, bn_step, step, coef[:, 0:MT, 0], coef[:, 0:MT, 1], mv, tmp,
                            pv("b1"), pv("g1"), pv("be1"), MT, sqrt_in, sqrt_out)
            nc.vector.memset(tmp[:, 2, 0:1], 0.0).then_inc(bn_done, 1)

            def lo(u, f):
                dve.wait_ge(hi_done, u * 4 + f + 1)
                nc.vector.tensor_tensor(v_lo[:, f, :, :], v_f[:, :, :], v_hi[:, f, :, :].bitcast(F32),
                                        ALU.subtract).then_inc(lo_done, 1)

            count = 0

            def then(ins):
                nonlocal count
                count += 1
                ins.then_inc(w_step, 1)
                dve.wait_ge(w_step, count)

            def split_w(f, k, g):
                then(nc.vector.tensor_copy(w_hi[:, k, f, :, :], w_f[k][:, g, :, :]))
                then(nc.vector.tensor_tensor(w_lo[:, k, f, :, :], w_f[k][:, g, :, :],
                                             w_hi[:, k, f, :, :].bitcast(F32), ALU.subtract))

            for k in range(MT):
                dve.wait_ge(w_in0[k], 16)
                split_w(0, k, 0)
            lo(0, 0)
            for k in range(MT):
                g0, g1, g2 = (w_f[k][:, g, :, :] for g in range(3))
                dve.wait_ge(w_in[k], 16)
                split_w(3, k, 2)
                then(nc.vector.tensor_tensor(g0, g0, g2, ALU.add))
                then(nc.vector.tensor_scalar(g0, g0, 0.5, None, ALU.mult))
                then(nc.vector.scalar_tensor_tensor(g2, g1, 0.5, g0, op0=ALU.mult, op1=ALU.add))
                then(nc.vector.scalar_tensor_tensor(g0, g1, -0.5, g0, op0=ALU.mult, op1=ALU.add))
                split_w(1, k, 2)
                lo(0, 1 + k)
            for k in range(MT):
                split_w(2, k, 0)
            lo(0, 3)

            def unit(u, last):
                out_rows = [y[:, m, bass.ds(u * 2 * COLS, 2 * COLS)].rearrange("p (r e w) -> p r e w", e=2, w=W)
                            for m in range(MT)]
                as_rows = lambda a: a.rearrange("p (r w) -> p r w", w=W)
                for f in range(4):
                    if f == 2:
                        for m in range(MT):
                            dve.wait_ge(m2_done, u * 2 + m + 1)
                            m1 = bank[1][m][:, 0:COLS]
                            nc.vector.tensor_tensor(t1[:, m, :], m1, m2_f[:, m, :], ALU.add).then_inc(t_done, 1)
                            nc.vector.tensor_tensor(t2[:, m, :], m1, m2_f[:, m, :], ALU.subtract).then_inc(t_done, 1)
                        for m in range(MT):
                            dve.wait_ge(t_done, u * 4 + 2 * m + 1)
                            nc.vector.tensor_tensor(out_rows[m][:, :, 0, :], as_rows(bank[0][m][:, 0:COLS]),
                                                    as_rows(t1[:, m, :]), ALU.add).then_inc(even_done, 1)
                    if f == 3:
                        dve.wait_ge(mm_done, u * 4 + 4)
                        dve.wait_ge(t_done, u * 4 + 4)
                        for m in range(MT):
                            nc.vector.tensor_tensor(out_rows[m][:, :, 1, :], as_rows(t2[:, m, :]),
                                                    as_rows(bank[3][m][:, 0:COLS]), ALU.subtract)\
                                .then_inc(odd_done, 1)
                    if not last:
                        lo(u + 1, f)
                for m in range(MT):
                    dve.wait_ge(odd_done, u * 2 + m + 1)
                    for e in range(2):
                        nc.vector.bn_stats(stats[:, m, bass.ds(u * 2 + e, 1), :].rearrange("p a b -> p (a b)"),
                                           y[:, m, bass.ds((u * 2 + e) * COLS, COLS)])

            over_units(dve, unit)

        @block.tensor
        def _(pe):
            ready = (2 * MT, 4 * MT + 8 * MT - 2 * MT, 12 * MT, 12 * MT)

            def unit(u, last):
                for f in range(4):
                    if isinstance(u, int) and u == 0:
                        pe.wait_ge(w_step, ready[f])
                    elif f == 0:
                        pe.wait_ge(even_done, u * 2)
                    pe.wait_ge(lo_done, u * 4 + f + 1)
                    for m in range(MT):
                        steps = [(w, v, k, b) for k in range(MT) for b in range(3)
                                 for w, v in ((w_hi, v_hi), (w_lo, v_hi), (w_hi, v_lo))]
                        for at, (w, v, k, b) in enumerate(steps):
                            rhs = v[:, f, k, :].rearrange("p (r w) -> p r w", w=W + 2)[:, :, b:b + W]
                            ins = nc.tensor.matmul(bank[f][m][:, 0:COLS], w[:, k, f, b, m * P:(m + 1) * P], rhs,
                                                   start=at == 0, stop=at == len(steps) - 1)
                    ins.then_inc(mm_done, 1)

            over_units(pe, unit)


def inner(v, r=0, c=0):
    return v.rearrange("p (i h w) -> p i h w", i=2, h=H + 2)[:, :, 1 + r:1 + r + H, 1 + c:1 + c + W]


def rows(v):
    return v.rearrange("p (i h w) -> p i h w", i=2, h=H)


def softplus_dve(nc, dve, sp, rs, step, exp_done, ln_done):
    col = lambda i: sp[:, i:i + 1]
    n = [0]

    def then(ins):
        n[0] += 1
        ins.then_inc(step, 1)
        dve.wait_ge(step, n[0])

    then(nc.vector.tensor_scalar(col(1), rs, -1.0, None, ALU.mult))
    then(nc.vector.tensor_tensor(col(1), col(1), rs, ALU.min))
    dve.wait_ge(exp_done, 1)
    then(nc.vector.tensor_scalar(col(3), col(2), 1.0, None, ALU.add))
    dve.wait_ge(ln_done, 1)
    then(nc.vector.tensor_scalar(col(5), col(3), -1.0, None, ALU.add))
    then(nc.vector.tensor_scalar(col(6), col(5), 0.0, None, ALU.is_equal))
    then(nc.vector.tensor_tensor(col(5), col(5), col(6), ALU.add))
    then(nc.vector.tensor_tensor(col(4), col(4), col(6), ALU.add))
    then(nc.vector.reciprocal(col(5), col(5)))
    then(nc.vector.tensor_tensor(col(4), col(4), col(5), ALU.mult))
    then(nc.vector.tensor_tensor(col(4), col(4), col(2), ALU.mult))
    then(nc.vector.tensor_scalar(col(0), rs, 0.0, None, ALU.max))
    then(nc.vector.tensor_tensor(col(0), col(0), col(4), ALU.add))


def softplus_act(nc, act, sp, step, exp_done, ln_done):
    act.wait_ge(step, 2)
    nc.scalar.activation(sp[:, 2:3], sp[:, 1:2], ACT.Exp).then_inc(exp_done, 1)
    act.wait_ge(step, 3)
    nc.scalar.activation(sp[:, 4:5], sp[:, 3:4], ACT.Ln).then_inc(ln_done, 1)


def conv3(nc, w3, y, stats, mv, tmp, coef, pv, y3_t):
    with ExitStack() as c:
        sb = lambda name, shape, dt: c.enter_context(nc.sbuf_tensor(name, shape, dt))
        sem = lambda name: c.enter_context(nc.semaphore(name))
        w_f = sb("c_w", [P, MT, C_IN], F32)
        w_hi = sb("c_w_hi", [P, MT, C_IN], F32R)
        w_lo = sb("c_w_lo", [P, MT, C_IN], F32R)
        z_f = sb("c_z", [P, 2, MT, COLS], F32)
        z_hi = sb("c_z_hi", [P, 2, MT, COLS], F32R)
        z_lo = sb("c_z_lo", [P, 2, MT, COLS], F32R)
        y3s = sb("c_y3", [P, 2, KT, COLS], F32)
        stats3 = sb("c_stats3", [P, KT, PAIRS, 6], F32)
        ps = c.enter_context(nc.psum_tensor("c_ps", [P, 8, 512], F32))
        w_in, w_split = [sem(f"c_w_in{k}") for k in range(MT)], sem("c_w_split")
        bn_step, sqrt_in, sqrt_out, bn_done = sem("c_bn_step"), sem("c_sqrt_in"), sem("c_sqrt_out"), sem("c_bn_done")
        z_done, lo_done = sem("c_z_done"), sem("c_lo_done")
        conv_done, y_done = sem("c_conv_done"), sem("c_y_done")
        stored = [sem(f"c_stored{s}") for s in range(2)]
        agg = sem("c_agg")
        block = c.enter_context(nc.Block())

        @block.sync
        def _(sync):
            for k in range(MT):
                sync.dma_start(w_f[:, k, :], w3[k * P:(k + 1) * P, :]).then_inc(w_in[k], 16)

            def body(i, last):
                for s in range(2):
                    sync.wait_ge(y_done, (i * 2 + s + 1) * KT)
                    sync.dma_start(y3_t[:, :, bass.ds((i * 2 + s) * COLS, COLS)], y3s[:, s, :, :])\
                        .then_inc(stored[s], 16)

            over_bodies(sync, body)
            for s in range(2):
                sync.wait_ge(stored[s], BODIES * 16)

        @block.scalar
        def _(act):
            act.wait_ge(sqrt_in, 1)
            nc.scalar.activation(tmp[:, 1, 0:MT], tmp[:, 0, 0:MT], ACT.Sqrt).then_inc(sqrt_out, 1)
            act.wait_ge(bn_done, 1)

            def z(n, s):
                for m in range(MT):
                    src = y[:, m, bass.ds(n * COLS, COLS)]
                    sc, sh = coef[:, m, 0:1], coef[:, m, 1:2]
                    nc.scalar.activation(z_f[:, s, m, :], src, ACT.Relu, bias=sh, scale=sc)
                    nc.scalar.activation(z_hi[:, s, m, :], src, ACT.Relu, bias=sh, scale=sc).then_inc(z_done, 1)

            for s in range(2):
                z(s, s)

            def body(i, first, last):
                for s in range(2):
                    if not first:
                        act.wait_ge(stored[s], i * 16)
                    for m in range(KT):
                        act.wait_ge(conv_done, (i * 2 + s) * KT + m + 1)
                        nc.scalar.activation(y3s[:, s, m, :], ps[:, 4 * s + m % 4, 0:COLS],
                                             ACT.Copy).then_inc(y_done, 1)
                    if not last:
                        z(i * 2 + s + 2, s)

            body(0, True, False)
            with act.Fori(1, BODIES - 1) as i:
                body(i, False, False)
            body(BODIES - 1, False, True)

        @block.vector
        def _(dve):
            step = 0
            for m in range(MT):
                nc.vector.bn_aggr(mv[:, m, :], stats[:, m, :, :].rearrange("p a b -> p (a b)")).then_inc(bn_step, 1)
                step += 1
            dve.wait_ge(bn_step, step)
            step = bn_coefficients(nc, dve, bn_step, step, coef[:, 0:MT, 0], coef[:, 0:MT, 1], mv, tmp,
                                   pv("b2"), pv("g2"), pv("be2"), MT, sqrt_in, sqrt_out)
            nc.vector.memset(tmp[:, 2, 0:1], 0.0).then_inc(bn_done, 1)
            for k in range(MT):
                dve.wait_ge(w_in[k], 16)
                split(nc, dve, w_hi[:, k, :], w_lo[:, k, :], w_f[:, k, :], w_split, 2 * k)

            def lo(n, s):
                dve.wait_ge(z_done, n * 2 + MT)
                nc.vector.tensor_tensor(z_lo[:, s, :, :], z_f[:, s, :, :], z_hi[:, s, :, :].bitcast(F32),
                                        ALU.subtract).then_inc(lo_done, 1)

            for s in range(2):
                lo(s, s)

            def body(i, last):
                for s in range(2):
                    for m in range(KT):
                        dve.wait_ge(y_done, (i * 2 + s) * KT + m + 1)
                        nc.vector.bn_stats(stats3[:, m, bass.ds(i * 2 + s, 1), :].rearrange("p a b -> p (a b)"),
                                           y3s[:, s, m, :])
                    if not last:
                        lo(i * 2 + s + 2, s)

            over_bodies(dve, body)
            nc.vector.memset(tmp[:, 3, 0:1], 0.0).then_inc(bn_step, 1)
            dve.wait_ge(bn_step, step + 1)
            for m in range(KT):
                nc.vector.bn_aggr(mv[:, m, :], stats3[:, m, :, :].rearrange("p a b -> p (a b)")).then_inc(agg, 1)

        @block.tensor
        def _(pe):
            pe.wait_ge(w_split, 2 * MT)

            def body(i, last):
                for s in range(2):
                    pe.wait_ge(lo_done, i * 2 + s + 1)
                    for m in range(KT):
                        if m >= 4:
                            pe.wait_ge(y_done, (i * 2 + s) * KT + m - 3)
                        steps = [(w, v, k) for k in range(MT) for w, v in ((w_hi, z_hi), (w_lo, z_hi), (w_hi, z_lo))]
                        for at, (w, v, k) in enumerate(steps):
                            last_mm = nc.tensor.matmul(ps[:, 4 * s + m % 4, 0:COLS], w[:, k, m * P:(m + 1) * P],
                                                       v[:, s, k, :], start=at == 0, stop=at == len(steps) - 1)
                        last_mm.then_inc(conv_done, 1)

            over_bodies(pe, body)


def diagonal(a, c, n, start):
    length, stride = a.shape[1], P - GC
    if c == KT - 1:
        parts = ((0, KT // 2, GC * c), (KT // 2, KT // 2, GC * c + KT // 2 * stride))
    else:
        parts = ((0, KT - 1 - c, P * (c + 1) + stride), (KT - 1 - c, c + 1, GC * c))
    for q, count, row in parts:
        first = a[row:row + 1, bass.ds(start, n)]
        yield q * GC, count * GC, bass.AP(a.tensor, first.offset, [[stride * length, count], [length, GC], [1, n]])


def later(at, d):
    p, i, s = at
    i, s = (i + 1, s) if d == 2 else (i + s, 1 - s)
    if isinstance(i, int) and i == BODIES:
        p, i = p + 1, 0
    return (p, i, s) if p < PASSES else None


def before(at):
    p, i, s = at
    if s:
        return p, i, 0
    if isinstance(i, int) and i == 0:
        return (p - 1, BODIES - 1, 1) if p else None
    return p, i - 1, 1


def over_steps(engine, step):
    for p in range(PASSES):
        for s in range(2):
            step((p, 0, s))
        with engine.Fori(1, BODIES - 1) as i:
            for s in range(2):
                step((p, i, s))
        for s in range(2):
            step((p, BODIES - 1, s))


def layer1(nc, x, x_t, y3, y3_t, out_t, sources, mv, tmp, coef, pv, sp):
    coef_dram = nc.dram_tensor("coef_spill", [2 * C_IN, 2], F32).ap()
    with ExitStack() as c:
        sb = lambda name, shape, dt: c.enter_context(nc.sbuf_tensor(name, shape, dt))
        sem = lambda name: c.enter_context(nc.semaphore(name))
        bank = lambda name: c.enter_context(nc.psum_tensor(name, [P, 512], F32))
        coef_sk = sb("d_coef_sk", [P, KT, 2], F32)
        w_raw = sb("d_w_raw", [P, WPP, P], F32)
        w_main_hi, w_main_lo, w_side, w_side_lo, w_out = (
            [sb(f"d_w_{name}{s}", [P, n, P], F32R) for s in range(2)]
            for name, n in (("main_hi", WPP), ("main_lo", WPP), ("side", WPP), ("side_lo", WPP // 2), ("out", WPP)))
        x_win = sb("d_x_win", [P, 2, WT, COLS], F32)
        y_win = sb("d_y_win", [P, 2, WT, COLS], F32)
        xy_res = sb("d_xy_res", [P, 2 * 4 * COLS], F32)
        x_res, y_res = (xy_res[:, n * 4 * COLS:(n + 1) * 4 * COLS].rearrange("p (s o n) -> p s o n", s=2, o=2)
                        for n in range(2))
        raw_bufs = (w_raw[:, :, :], xy_res[:, 0:WPP * P].rearrange("p (g m) -> p g m", m=P))
        raw_at = lambda p, stage: stage % 2 if p == 0 else 0
        v_hi = sb("d_v_hi", [P, 2, WT, PAD], F32R)
        v_lo = sb("d_v_lo", [P, 2, WT, PAD], F32R)
        low = sb("d_low", [P, 2, 2, PAD], F32R)
        upp = sb("d_upp", [P, 2, 2, PAD], F32R)
        low3 = sb("d_low3", [P, 2, 2, PAD], F32R)
        upp3 = sb("d_upp3", [P, 2, 2, PAD], F32R)
        h_f = sb("d_h", [P, BANKS, COLS], F32)
        h_hi = sb("d_h_hi", [P, HB, COLS], F32R)
        h_lo = sb("d_h_lo", [P, HB, COLS], F32R)
        part = sb("d_part", [P, 2, COLS], F32)
        res = sb("d_res", [P, 4, COLS], F32)
        hid = [bank(f"d_hid{b}") for b in range(BANKS)]
        acc = [[bank(f"d_acc{oo}{h}") for h in range(2)] for oo in range(2)]

        raw_in = [sem(f"d_raw_in{n}") for n in range(2)]
        w_step, pads_done, zeros_done = (sem(f"d_{n}") for n in ("w_step", "pads_done", "zeros_done"))
        coef_out, sk_in, bn_step, sqrt_in, sqrt_out, bn_done = (
            sem(f"d_{n}") for n in ("coef_out", "sk_in", "bn_step", "sqrt_in", "sqrt_out", "bn_done"))
        win_in, res_in, low_in, upp_in, low3_in, upp3_in = (
            [sem(f"d_{n}_in{s}") for s in range(2)] for n in ("win", "res", "low", "upp", "low3", "upp3"))
        win_sum, win_relu, win_lo = sem("d_win_sum"), sem("d_win_relu"), sem("d_win_lo")
        res_scaled, res_sum, res_relu = sem("d_res_scaled"), sem("d_res_sum"), sem("d_res_relu")
        first_done, h_done, hi_done, lo_done = (
            sem(f"d_{n}") for n in ("first_done", "h_done", "hi_done", "lo_done"))
        oct_done, part_done, comb_done, fin_done = (
            sem(f"d_{n}") for n in ("oct_done", "part_done", "comb_done", "fin_done"))
        stored = [sem(f"d_stored{o}") for o in range(4)]
        block = c.enter_context(nc.Block())

        number = lambda at: at[1] * 2 + (at[0] * PAIRS + at[2])
        pair = lambda at: at[1] * 2 + at[2]
        fills = lambda at: at[1] + (at[0] * BODIES + 1)

        @block.sync
        def _(sync):
            def load_window(at):
                p, _, s = at
                third = (2 * p + 2) % KT
                cols = bass.ds(pair(at) * COLS, COLS)
                for dst, src in ((x_win, x_t), (y_win, y3_t)):
                    sync.dma_start(dst[:, s, 0:2, :], src[:, 2 * p:2 * p + 2, cols]).then_inc(win_in[s], 16)
                    sync.dma_start(dst[:, s, 2, :], src[:, third, cols]).then_inc(win_in[s], 16)

            def load_residual(at):
                p, _, s = at
                for oo in range(2):
                    for dst, src in ((x_res, x), (y_res, y3)):
                        for first, count, pattern in diagonal(src, 2 * p + oo, COLS, pair(at) * COLS):
                            sync.dma_start(dst[first:first + count, s, oo, :], pattern).then_inc(res_in[s], 16)

            def load_stacks(at):
                s = at[2]
                sync.wait_ge(win_lo, (number(at) + 1) * WT)
                for dst, done, row, t, parts in ((low3, low3_in, 0, 1, (v_hi, v_hi, v_lo)),
                                                 (low, low_in, 0, 1, (v_hi, v_lo)),
                                                 (upp, upp_in, P // 2, 0, (v_hi, v_lo)),
                                                 (upp3, upp3_in, P - QUARTER, 0, (v_hi, v_hi, v_lo))):
                    size = QUARTER if len(parts) == 3 else P // 2
                    for n, src in enumerate(parts):
                        sync.dma_start(dst[n * size:(n + 1) * size, s, :, :].bitcast(F32),
                                       src[row:row + size, s, t:t + 2, :].bitcast(F32)).then_inc(done[s], 16)

            def load_raw(p, stage):
                dst = raw_bufs[raw_at(p, stage)]
                last = p * STAGES + stage - (1 if p and (p, stage) > (1, 0) else 2)
                if last >= 0:
                    sync.wait_ge(w_step, (last + 1) * STEPS)
                if stage < 2:
                    parts = ((dst, sources[stage], p * WPP),)
                else:
                    parts = ((dst[:, n * OCT:(n + 1) * OCT, :], sources[2 + n], p * WPP + (stage - 2) * OCT)
                             for n in range(2))
                for to, src, first in parts:
                    n = to.shape[1]
                    sync.dma_start(to, src[:, first * P:(first + n) * P].rearrange("p (g m) -> p g m", m=P))\
                        .then_inc(raw_in[raw_at(p, stage)], 16)

            def store(at, oo):
                o = 2 * at[2] + oo
                sync.wait_ge(fin_done, number(at) * 2 + oo + 1)
                sync.dma_start(out_t[:, 2 * at[0] + oo, bass.ds(pair(at) * COLS, COLS)], res[:, o, :])\
                    .then_inc(stored[o], 16)

            load_window((0, 0, 0))
            load_raw(0, 0)
            load_raw(0, 1)
            sync.wait_ge(bn_done, 1)
            for copy, done in ((0, stored[3]), (1, coef_out)):
                sync.dma_start(coef_dram[copy * C_IN:(copy + 1) * C_IN, :].rearrange("(t p) a -> p t a", p=P),
                               coef[:, :, :]).then_inc(done, 16)
            load_stacks((0, 0, 0))
            load_raw(0, 2)
            for done in (stored[3], coef_out):
                sync.wait_ge(done, 16)
            for c in range(KT):
                first = coef_dram[P * (c + 1) + P - GC:P * (c + 2), :]
                sync.dma_start(coef_sk[:, c, :], bass.AP(coef_dram.tensor, first.offset,
                                                         [[2 * (P - GC), OCT], [2, GC], [1, 2]])).then_inc(sk_in, 16)
            load_window((0, 0, 1))
            load_raw(0, 3)

            def step(at):
                p, i, s = at
                prepare = isinstance(i, int) and p + 1 < PASSES
                if prepare and i == 0:
                    load_raw(p + 1, s)
                if (then := later(at, 2)) is not None:
                    sync.wait_ge(win_lo, (number(at) + 1) * WT)
                    load_window(then)
                then = later(at, 1)
                if then is not None:
                    load_stacks(then)
                if before(at) is None:
                    sync.wait_ge(w_step, STAGES * STEPS)
                    load_residual(at)
                if (prev := before(at)) is not None:
                    store(prev, 1)
                if then is not None:
                    load_residual(then)
                store(at, 0)
                if prepare and (i, s) in ((0, 1), (BODIES - 1, 0)):
                    load_raw(p + 1, 3 - s)

            over_steps(sync, step)
            store((PASSES - 1, BODIES - 1, 1), 1)
            for o in range(4):
                sync.wait_ge(stored[o], 16 * (PASSES * BODIES + (o == 3)))

        @block.gpsimd
        def _(pool):
            nc.gpsimd.memset(v_hi[:, :, :, :].bitcast(F32), 0.0).then_inc(pads_done, 1)
            nc.gpsimd.memset(v_lo[:, :, :, :].bitcast(F32), 0.0).then_inc(pads_done, 1)

            def window_lo(at, t):
                s = at[2]
                pool.wait_ge(win_relu, number(at) * WT + t + 1)
                nc.gpsimd.tensor_tensor(inner(v_lo[:, s, t, :]), rows(x_win[:, s, t, :]),
                                        inner(v_hi[:, s, t, :]).bitcast(F32), ALU.subtract).then_inc(win_lo, 1)

            def residual_sum(at, oo):
                s = at[2]
                pool.wait_ge(res_scaled, number(at) * 2 + oo + 1)
                nc.gpsimd.tensor_tensor(y_res[:, s, oo, :], y_res[:, s, oo, :], x_res[:, s, oo, :],
                                        ALU.add).then_inc(res_sum, 1)

            def finish(at, oo):
                o = 2 * at[2] + oo
                pool.wait_ge(comb_done, number(at) * 2 + oo + 1)
                pool.wait_ge(res_relu, number(at) * 2 + oo + 1)
                nc.gpsimd.tensor_tensor(res[:, o, :], res[:, o, :], x_res[:, at[2], oo, :],
                                        ALU.add).then_inc(fin_done, 1)

            pool.wait_ge(pads_done, 2)
            for t in range(WT):
                window_lo((0, 0, 0), t)
            pool.wait_ge(win_lo, WT)
            for tile in (low3, upp3):
                nc.gpsimd.memset(tile[3 * QUARTER:P, :, :, :].bitcast(F32), 0.0).then_inc(zeros_done, 1)
            pool.wait_ge(zeros_done, 2)

            def step(at):
                if (then := later(at, 1)) is not None:
                    for t in range(WT):
                        window_lo(then, t)
                for oo in range(2):
                    residual_sum(at, oo)
                if (prev := before(at)) is not None:
                    finish(prev, 1)
                finish(at, 0)

            over_steps(pool, step)
            finish((PASSES - 1, BODIES - 1, 1), 1)

        @block.scalar
        def _(act):
            act.wait_ge(sqrt_in, 1)
            nc.scalar.activation(tmp[:, 1, :], tmp[:, 0, :], ACT.Sqrt).then_inc(sqrt_out, 1)
            act.wait_ge(bn_done, 1)
            act.wait_ge(pads_done, 1)

            def window_tile(at, t):
                p, _, s = at
                shift = coef[:, (2 * p + t) % KT, 1:2]
                act.wait_ge(win_sum, number(at) * WT + t + 1)
                nc.scalar.activation(inner(v_hi[:, s, t, :]), rows(y_win[:, s, t, :]), ACT.Relu, bias=shift)
                nc.scalar.activation(x_win[:, s, t, :], y_win[:, s, t, :], ACT.Relu, bias=shift).then_inc(win_relu, 1)

            def residual_scale(at, oo):
                p, _, s = at
                if before(at) is None and oo == 0:
                    act.wait_ge(sk_in, KT * 16)
                act.wait_ge(res_in[s], fills(at) * 128)
                sc, sh = (coef_sk[:, 2 * p + oo, n:n + 1] for n in range(2))
                nc.scalar.activation(y_res[:, s, oo, :], y_res[:, s, oo, :], ACT.Identity, bias=sh,
                                     scale=sc).then_inc(res_scaled, 1)

            def residual_relu(at, oo):
                p, _, s = at
                act.wait_ge(res_sum, number(at) * 2 + oo + 1)
                nc.scalar.activation(x_res[:, s, oo, :], y_res[:, s, oo, :], ACT.Relu).then_inc(res_relu, 1)

            def move_low_parts(at, oo):
                act.wait_ge(oct_done, number(at) * 2 + oo + 1)
                nc.scalar.activation(part[P // 2:P, oo, :], acc[oo][0][0:P // 2, 0:COLS], ACT.Copy)
                nc.scalar.activation(part[0:P // 2, oo, :], acc[oo][1][P // 2:P, 0:COLS], ACT.Copy)\
                    .then_inc(part_done, 1)

            for t in range(WT):
                window_tile((0, 0, 0), t)

            def step(at):
                p = at[0]
                hb = pv("hid_b")
                window_at, scale_at, relu_at = (4, 13, 15) if before(at) is None else (0, 3, 9)
                for g in range(WPP):
                    k, b = p * WPP + g, g % BANKS
                    act.wait_ge(first_done, number(at) * WPP + g + 1)
                    if g >= BANKS or before(at) is not None:
                        act.wait_ge(lo_done, number(at) * (WPP // 2) + g // 2 - BANKS // 2 + 1)
                    nc.scalar.activation(h_f[:, b, :], hid[b][:, 0:COLS], ACT.Relu,
                                         bias=hb[:, k:k + 1]).then_inc(h_done, 1)
                    if 0 <= g - window_at < WT and (then := later(at, 1)) is not None:
                        window_tile(then, g - window_at)
                    if g == scale_at:
                        residual_scale(at, 0)
                        residual_scale(at, 1)
                    if g == relu_at:
                        residual_relu(at, 0)
                        residual_relu(at, 1)
                    if g == 5 and (prev := before(at)) is not None:
                        move_low_parts(prev, 1)
                    if g == 13:
                        move_low_parts(at, 0)

            over_steps(act, step)
            move_low_parts((PASSES - 1, BODIES - 1, 1), 1)

        @block.vector
        def _(dve):
            bn_coefficients(nc, dve, bn_step, 0, coef[:, :, 0], coef[:, :, 1], mv, tmp, pv("b3"), pv("g3"),
                            pv("be3"), KT, sqrt_in, sqrt_out, by=sp[:, 0:1])
            nc.vector.memset(sp[:, 7:8], 0.0).then_inc(bn_done, 1)

            def window_sum(at, t):
                p, _, s = at
                dve.wait_ge(win_in[s], fills(at) * 64)
                nc.vector.scalar_tensor_tensor(y_win[:, s, t, :], y_win[:, s, t, :], coef[:, (2 * p + t) % KT, 0:1],
                                               x_win[:, s, t, :], op0=ALU.mult, op1=ALU.add).then_inc(win_sum, 1)

            def combine(at, oo):
                p, _, s = at
                o = 2 * s + oo
                dve.wait_ge(part_done, number(at) * 2 + oo + 1)
                if o == 3:
                    dve.wait_ge(stored[o], fills(at) * 16)
                elif not (isinstance(at[1], int) and p == at[1] == 0):
                    dve.wait_ge(stored[o], fills(at) * 16 - 16)
                for half, h in ((slice(P // 2, P), 0), (slice(0, P // 2), 1)):
                    ins = nc.vector.scalar_tensor_tensor(
                        res[half, o, :], acc[oo][h][half, 0:COLS], pv("out_b")[half, 2 * p + oo:2 * p + oo + 1],
                        part[half, oo, :], op0=ALU.add, op1=ALU.add)
                ins.then_inc(comb_done, 1)

            def weights(p, stage, n):
                b, count = p % 2, (p * STAGES + stage) * STEPS + n
                raw = raw_bufs[raw_at(p, stage)]
                octets = lambda a: a.rearrange("p (o j) m -> p o j m", o=2)
                if count:
                    dve.wait_ge(w_step, count)
                if n == 0:
                    loads = 3 + 6 * (p - 1) + (1, 2, 4, 6)[stage] if p else (1, 1, 3, 3)[stage]
                    dve.wait_ge(raw_in[raw_at(p, stage)], 16 * loads)
                if stage == 0:
                    half = slice(n // 2 * OCT, (n // 2 + 1) * OCT)
                    raw, hi, lo = raw[:, half, :], w_main_hi[b][:, half, :], w_main_lo[b][:, half, :]
                    if n % 2 == 0:
                        ins = nc.vector.tensor_copy(hi, raw)
                    else:
                        ins = nc.vector.tensor_tensor(lo, raw, hi.bitcast(F32), ALU.subtract)
                elif stage == 1 and n == 0:
                    ins = nc.vector.tensor_copy(w_side[b][:, :, :], raw)
                elif stage == 1:
                    hi, js = octets(w_side[b][:, :, :]), (slice(2, 6), slice(0, 2), slice(6, 8))[n - 1]
                    at = slice(0, P) if n == 1 else slice(QUARTER, 2 * QUARTER)
                    lo = octets(w_side_lo[b][:, :, :]) if n == 1 else hi[at, :, js, :]
                    ins = nc.vector.tensor_tensor(lo, octets(raw)[at, :, js, :], hi[at, :, js, :].bitcast(F32),
                                                  ALU.subtract)
                else:
                    w = w_out[b][:, (stage - 2) * OCT:(stage - 1) * OCT, :]
                    raw_a, raw_b = raw[:, 0:OCT, :], raw[:, OCT:2 * OCT, :]
                    if n == 0:
                        ins = nc.vector.tensor_copy(w, raw_b)
                    elif n == 1:
                        ins = nc.vector.tensor_tensor(raw_b, raw_b, w.bitcast(F32), ALU.subtract)
                    elif n == 2:
                        ins = nc.vector.tensor_copy(w, raw_a)
                    else:
                        ins = nc.vector.tensor_tensor(w, w.bitcast(F32), raw_b, ALU.add)
                ins.then_inc(w_step, 1)

            for t in range(WT):
                window_sum((0, 0, 0), t)
            for stage in range(STAGES - 1):
                for n in range(STEPS):
                    weights(0, stage, n)

            def step(at):
                p, i, s = at
                for g in range(0, WPP, 2):
                    b, f = g % HB, g % BANKS
                    count = number(at) * (WPP // 2) + g // 2 + 1
                    dve.wait_ge(h_done, number(at) * WPP + g + 2)
                    nc.vector.tensor_copy(h_hi[:, b:b + 2, :], h_f[:, f:f + 2, :]).then_inc(hi_done, 1)
                    if g == 6 and (prev := before(at)) is not None:
                        combine(prev, 1)
                    if before(at) is None and 2 <= g <= 8:
                        if g == 2:
                            for t in range(WT):
                                window_sum((0, 0, 1), t)
                        weights(0, STAGES - 1, g // 2 - 1)
                    if g in (10, 12, 14) and (then := later(at, 2)) is not None:
                        window_sum(then, g // 2 - 5)
                    if g == 14:
                        combine(at, 0)
                    if isinstance(i, int) and p + 1 < PASSES and g in W_AT:
                        weights(p + 1, s if i == 0 else 2 + s, W_AT.index(g))
                    dve.wait_ge(hi_done, count)
                    nc.vector.tensor_tensor(h_lo[:, b:b + 2, :], h_f[:, f:f + 2, :],
                                            h_hi[:, b:b + 2, :].bitcast(F32), ALU.subtract).then_inc(lo_done, 1)

            over_steps(dve, step)
            combine((PASSES - 1, BODIES - 1, 1), 1)

        @block.tensor
        def _(pe):
            def first_product(at, g):
                p, i, s = at
                b, k = p % 2, p * WPP + g
                oo, j = divmod(g, OCT)
                quarter = j in (0, 1, 6, 7)
                if g == 0:
                    if isinstance(i, int) and (i, s) == (0, 0):
                        pe.wait_ge(w_step, (p * STAGES + 2) * STEPS)
                    pe.wait_ge(win_lo, (number(at) + 1) * WT)
                if g in (0, 6) and before(at) is None:
                    pe.wait_ge(zeros_done, 1 if g == 0 else 2)
                if g in (0, 2, 4, 6):
                    pe.wait_ge((low3_in, low_in, upp_in, upp3_in)[g // 2][s], fills(at) * (48 if quarter else 32))
                if g >= BANKS or before(at) is not None:
                    pe.wait_ge(h_done, number(at) * WPP + g - BANKS + 1)
                if j < OCT // 2:
                    main, side, main_tile, side_tile = oo, low3 if quarter else low, 0, 1
                else:
                    main, side, main_tile, side_tile = oo + 1, upp3 if quarter else upp, 1, 0
                at_main, at_side = (SHIFTS[shift_of(k, t)] for t in (main_tile, side_tile))
                products = [(w_main_hi, g, v_hi[:, s, main, :], at_main), (w_main_lo, g, v_hi[:, s, main, :], at_main),
                            (w_main_hi, g, v_lo[:, s, main, :], at_main), (w_side, g, side[:, s, oo, :], at_side)]
                if not quarter:
                    products.append((w_side_lo, 4 * oo + j - 2, side[:, s, oo, :], at_side))
                for n, (w, at_w, v, shift) in enumerate(products):
                    ins = nc.tensor.matmul(hid[g % BANKS][:, 0:COLS], w[b][:, at_w, :], inner(v, *shift),
                                           start=n == 0, stop=n == len(products) - 1)
                ins.then_inc(first_done, 1)

            def second_product(at, g):
                p = at[0]
                oo, j = divmod(g, OCT)
                if j == 0 and isinstance(at[1], int) and at[1] == at[2] == 0:
                    pe.wait_ge(w_step, (p * STAGES + 3 + oo) * STEPS)
                pe.wait_ge(lo_done, number(at) * (WPP // 2) + g // 2 + 1)
                h, q = divmod(j, OCT // 2)
                for n, v in enumerate((h_hi, h_lo)):
                    ins = nc.tensor.matmul(acc[oo][h][:, 0:COLS], w_out[p % 2][:, g, :], v[:, g % HB, :],
                                           start=q == n == 0, stop=q == OCT // 2 - 1 and n == 1)
                if j == OCT - 1:
                    ins.then_inc(oct_done, 1)

            for g in range(LAG):
                first_product((0, 0, 0), g)

            def step(at):
                for g in range(0, WPP, 2):
                    for g1 in (g + LAG, g + LAG + 1):
                        if g1 < WPP:
                            first_product(at, g1)
                        elif (then := later(at, 1)) is not None:
                            first_product(then, g1 - WPP)
                    second_product(at, g)
                    second_product(at, g + 1)

            over_steps(pe, step)


def window_weights(w1, w2, b2):
    main, side, out_a, out_b = (np.zeros((GROUPS, P, P), w1.dtype) for _ in range(4))
    bias = np.zeros((P, KT), b2.dtype)
    for k in range(GROUPS):
        m, (c, j) = group_of(k), divmod(k, OCT)
        w, cut = w1[m].T, P - GC * j
        if j < OCT // 2:
            main[k, GC * j:] = w[:cut]
            rest, first = w[cut:], 0
        else:
            main[k, :GC * (j + 1)] = w[cut:]
            rest, first = w[:cut], -cut
        size = QUARTER if len(rest) <= QUARTER else P // 2
        for start in range(0, 3 * QUARTER, size):
            at = start + first % size
            side[k, at:at + len(rest)] = rest
        q = GC * (OCT - 1 - j)
        out_a[k, :, q:q + GC] = w2[m].T
        out_b[k, :, (q + P // 2) % P:(q + P // 2) % P + GC] = w2[m].T
        bias[q:q + GC, c] = b2[GC * m:GC * (m + 1)]
    by_row = lambda a: np.ascontiguousarray(a.transpose(1, 0, 2)).reshape(P, GROUPS * P)
    return by_row(main), by_row(side), by_row(out_a), by_row(out_b), bias


def kernel(x, L0_conv_w1, L0_conv_b1, L0_conv_g1, L0_conv_be1, L0_conv_w2, L0_conv_b2, L0_conv_g2, L0_conv_be2,
           L0_conv_w3, L0_conv_b3, L0_conv_g3, L0_conv_be3, L0_conv_residual_scale, L1_conv_w1, L1_conv_b1,
           L1_conv_w2, L1_conv_b2):
    import concourse.bacc as bacc
    from concourse.bass_utils import run_bass_kernel_spmd

    wmain, wside, wout_a, wout_b, out_b = window_weights(np.asarray(L1_conv_w1), np.asarray(L1_conv_w2),
                                                         np.asarray(L1_conv_b2))
    by_tile = lambda a: np.asarray(a).reshape(-1, P).T
    hid_b = np.asarray(L1_conv_b1).reshape(GROUPS, HID)[[group_of(k) for k in range(GROUPS)]].T
    vectors = [by_tile(a) for a in (L0_conv_b1, L0_conv_g1, L0_conv_be1, L0_conv_b2, L0_conv_g2, L0_conv_be2,
                                    L0_conv_b3, L0_conv_g3, L0_conv_be3)]
    vectors += [np.repeat(np.asarray(L0_conv_residual_scale).reshape(1, 1), P, 0), hid_b, out_b]
    arrays = {
        "x": np.asarray(x).transpose(1, 0, 2, 3).reshape(C_IN, T),
        "w1": np.asarray(L0_conv_w1).reshape(C_MID, C_IN).T,
        "w2": np.asarray(L0_conv_w2).reshape(C_MID, C_MID, 9).transpose(1, 2, 0),
        "w3": np.asarray(L0_conv_w3).reshape(C_IN, C_MID).T,
        "wmain": wmain, "wside": wside, "wout_a": wout_a, "wout_b": wout_b,
        "params": np.concatenate(vectors, axis=1),
    }
    arrays = {f"{name}_dram": np.ascontiguousarray(a) for name, a in arrays.items()}
    nc = bacc.Bacc("TRN2", target_bir_lowering=False, num_devices=1)
    args = [nc.dram_tensor(name, a.shape, mybir.dt.from_np(a.dtype), kind="ExternalInput").ap()
            for name, a in arrays.items()]
    out = nc.dram_tensor("out_dram", [C_IN, T], F32, kind="ExternalOutput").ap()
    build(nc, *args, out)
    got = run_bass_kernel_spmd(nc, [arrays], core_ids=[0]).results[0]["out_dram"]
    got = np.asarray(got).reshape(KT, OCT, GC, N_IMG, H, W)
    result = np.empty((KT, OCT, GC, N_IMG, H, W), got.dtype)
    for c in range(KT):
        for q in range(OCT):
            result[(c - OCT + 1 + q) % KT, OCT - 1 - q] = got[c, q]
    return np.ascontiguousarray(result.reshape(C_IN, N_IMG, H, W).transpose(1, 0, 2, 3))
```
